# Optimizing a Trainium2 kernel written in Bass

```python
import numpy as np
import jax
import jax.numpy as jnp

def _softmax(x, axis=-1):
    return jax.nn.softmax(x, axis=axis)

def _gelu(x):
    return jax.nn.gelu(x, approximate=True)

def _silu(x):
    return jax.nn.silu(x)

def _sigmoid(x):
    return jax.nn.sigmoid(x)

def _layernorm(x, axis=-1, eps=1e-05):
    m = jnp.mean(x, axis=axis, keepdims=True)
    v = jnp.var(x, axis=axis, keepdims=True)
    return (x - m) / jnp.sqrt(v + eps)

def _scatter_add(tgt, idx, src, axis=0):
    return tgt.at[idx].add(src)

def _segment_sum(src, seg, n):
    return jax.ops.segment_sum(src, seg, n)
kernel_name = 'mk_macaron_d1_jaxref_r8_5f720b'

def setup_inputs(seed: int=0):
    np.random.seed(seed)
    _w = jnp.asarray

    def _L0_attn_setup():
        import jax, jax.numpy as jnp
        import numpy as np
        D_MODEL = 128
        EXPAND = 2
        D_INNER = EXPAND * D_MODEL
        D_STATE = 128
        D_CONV = 4
        NHEADS = 32
        NGROUPS = 1
        HEADDIM = D_INNER // NHEADS
        D_PROJ = 2 * D_INNER + 2 * NGROUPS * D_STATE + NHEADS
        EPS = 1e-05

        def _rmsnorm(y, w):
            return y * jax.lax.rsqrt(jnp.mean(y * y, axis=-1, keepdims=True) + EPS) * w

        def _forward(x, in_proj_w, conv_w, conv_b, A_log, Dp, dt_bias, norm_w, out_proj_w):
            B, T, _ = x.shape
            hpg = NHEADS // NGROUPS
            proj = jnp.einsum('btd,pd->btp', x, in_proj_w)
            s1 = D_INNER
            s2 = 2 * D_INNER
            s3 = s2 + NGROUPS * D_STATE
            s4 = s3 + NGROUPS * D_STATE
            x_ssm, z, B_in, C_in, dt_in = jnp.split(proj, [s1, s2, s3, s4], axis=-1)
            xc = jax.lax.conv_general_dilated(x_ssm.transpose(0, 2, 1), conv_w, window_strides=(1,), padding=[(D_CONV - 1, 0)], dimension_numbers=('NCH', 'OIH', 'NCH'), feature_group_count=D_INNER)
            xc = xc + conv_b[None, :, None]
            x_ssm = jax.nn.silu(xc.transpose(0, 2, 1))
            x_heads = x_ssm.reshape(B, T, NHEADS, HEADDIM)
            B_g = B_in.reshape(B, T, NGROUPS, D_STATE)
            C_g = C_in.reshape(B, T, NGROUPS, D_STATE)
            B_h = jnp.repeat(B_g, hpg, axis=2)
            C_h = jnp.repeat(C_g, hpg, axis=2)
            dt = jax.nn.softplus(dt_in + dt_bias)
            A = -jnp.exp(A_log)
            A_bar = jnp.exp(A * dt)

            def step(h, inp):
                ab, dtt, bt, ct, xt = inp
                h = ab[..., None, None] * h + (dtt[..., None] * bt)[:, :, None, :] * xt[..., None]
                y = jnp.einsum('bhn,bhpn->bhp', ct, h)
                return (h, y)
            h0 = jnp.zeros((B, NHEADS, HEADDIM, D_STATE), dtype=x.dtype)
            xs = (A_bar.transpose(1, 0, 2), dt.transpose(1, 0, 2), B_h.transpose(1, 0, 2, 3), C_h.transpose(1, 0, 2, 3), x_heads.transpose(1, 0, 2, 3))
            _, y_t = jax.lax.scan(step, h0, xs)
            y = y_t.transpose(1, 0, 2, 3)
            y = y + Dp[None, None, :, None] * x_heads
            y = y.reshape(B, T, D_INNER)
            y = _rmsnorm(y, norm_w) * jax.nn.silu(z)
            return jnp.einsum('bti,di->btd', y, out_proj_w)
        key = jax.random.key(seed)
        ks = jax.random.split(key, 8)
        B, T = (2, 256)
        x = jax.random.normal(ks[0], (B, T, D_MODEL), dtype=jnp.float32)
        in_proj_w = jax.random.normal(ks[1], (D_PROJ, D_MODEL), dtype=jnp.float32) * D_MODEL ** (-0.5)
        conv_w = jax.random.normal(ks[2], (D_INNER, 1, D_CONV), dtype=jnp.float32) * 0.3
        conv_b = jax.random.normal(ks[3], (D_INNER,), dtype=jnp.float32) * 0.02
        A_log = jax.random.normal(ks[4], (NHEADS,), dtype=jnp.float32) * 0.1
        Dp = jnp.ones((NHEADS,), dtype=jnp.float32)
        dt_bias = jax.random.normal(ks[5], (NHEADS,), dtype=jnp.float32) * 0.1
        norm_w = jnp.ones((D_INNER,), dtype=jnp.float32)
        out_proj_w = jax.random.normal(ks[6], (D_MODEL, D_INNER), dtype=jnp.float32) * D_INNER ** (-0.5)
        return {'x': x, 'in_proj_w': in_proj_w, 'conv_w': conv_w, 'conv_b': conv_b, 'A_log': A_log, 'Dp': Dp, 'dt_bias': dt_bias, 'norm_w': norm_w, 'out_proj_w': out_proj_w}
    _L0_attn_in = _L0_attn_setup()

    def _L0_ffn_setup():
        import jax, jax.numpy as jnp
        import numpy as np
        B, S, K, N = (8, 1024, 128, 128)
        key = jax.random.key(seed)
        k1, k2, k3, k4 = jax.random.split(key, 4)
        x = jax.random.normal(k1, (B, S, K), dtype=jnp.float32)
        CB = jnp.clip(jnp.round(jax.random.normal(k2, (N, K), dtype=jnp.float32) * 42.0), -127.0, 127.0)
        SCB = jax.random.uniform(k3, (N,), dtype=jnp.float32, minval=0.5, maxval=2.0)
        bias = jax.random.normal(k4, (N,), dtype=jnp.float32) * 0.02
        return {'x': x, 'CB': CB, 'SCB': SCB, 'bias': bias}
    _L0_ffn_in = _L0_ffn_setup()
    _d = {'L0_attn_x': _L0_attn_in['x'], 'L0_attn_in_proj_w': _L0_attn_in['in_proj_w'], 'L0_attn_conv_w': _L0_attn_in['conv_w'], 'L0_attn_conv_b': _L0_attn_in['conv_b'], 'L0_attn_A_log': _L0_attn_in['A_log'], 'L0_attn_Dp': _L0_attn_in['Dp'], 'L0_attn_dt_bias': _L0_attn_in['dt_bias'], 'L0_attn_norm_w': _L0_attn_in['norm_w'], 'L0_attn_out_proj_w': _L0_attn_in['out_proj_w'], 'L0_ffn_CB': _L0_ffn_in['CB'], 'L0_ffn_SCB': _L0_ffn_in['SCB'], 'L0_ffn_bias': _L0_ffn_in['bias']}
    _x0 = _d['L0_attn_x']
    _d['L0_attn_x'] = jax.random.normal(jax.random.fold_in(jax.random.key(seed), 1), (8, 512, 128), dtype=_x0.dtype)
    del _x0
    return _d

def reference(L0_attn_x, L0_attn_in_proj_w, L0_attn_conv_w, L0_attn_conv_b, L0_attn_A_log, L0_attn_Dp, L0_attn_dt_bias, L0_attn_norm_w, L0_attn_out_proj_w, L0_ffn_CB, L0_ffn_SCB, L0_ffn_bias):

    def _L0_attn_ref(x, in_proj_w, conv_w, conv_b, A_log, Dp, dt_bias, norm_w, out_proj_w):
        import jax, jax.numpy as jnp
        import numpy as np
        D_MODEL = 128
        EXPAND = 2
        D_INNER = EXPAND * D_MODEL
        D_STATE = 128
        D_CONV = 4
        NHEADS = 32
        NGROUPS = 1
        HEADDIM = D_INNER // NHEADS
        D_PROJ = 2 * D_INNER + 2 * NGROUPS * D_STATE + NHEADS
        EPS = 1e-05

        def _rmsnorm(y, w):
            return y * jax.lax.rsqrt(jnp.mean(y * y, axis=-1, keepdims=True) + EPS) * w

        def _forward(x, in_proj_w, conv_w, conv_b, A_log, Dp, dt_bias, norm_w, out_proj_w):
            B, T, _ = x.shape
            hpg = NHEADS // NGROUPS
            proj = jnp.einsum('btd,pd->btp', x, in_proj_w)
            s1 = D_INNER
            s2 = 2 * D_INNER
            s3 = s2 + NGROUPS * D_STATE
            s4 = s3 + NGROUPS * D_STATE
            x_ssm, z, B_in, C_in, dt_in = jnp.split(proj, [s1, s2, s3, s4], axis=-1)
            xc = jax.lax.conv_general_dilated(x_ssm.transpose(0, 2, 1), conv_w, window_strides=(1,), padding=[(D_CONV - 1, 0)], dimension_numbers=('NCH', 'OIH', 'NCH'), feature_group_count=D_INNER)
            xc = xc + conv_b[None, :, None]
            x_ssm = jax.nn.silu(xc.transpose(0, 2, 1))
            x_heads = x_ssm.reshape(B, T, NHEADS, HEADDIM)
            B_g = B_in.reshape(B, T, NGROUPS, D_STATE)
            C_g = C_in.reshape(B, T, NGROUPS, D_STATE)
            B_h = jnp.repeat(B_g, hpg, axis=2)
            C_h = jnp.repeat(C_g, hpg, axis=2)
            dt = jax.nn.softplus(dt_in + dt_bias)
            A = -jnp.exp(A_log)
            A_bar = jnp.exp(A * dt)

            def step(h, inp):
                ab, dtt, bt, ct, xt = inp
                h = ab[..., None, None] * h + (dtt[..., None] * bt)[:, :, None, :] * xt[..., None]
                y = jnp.einsum('bhn,bhpn->bhp', ct, h)
                return (h, y)
            h0 = jnp.zeros((B, NHEADS, HEADDIM, D_STATE), dtype=x.dtype)
            xs = (A_bar.transpose(1, 0, 2), dt.transpose(1, 0, 2), B_h.transpose(1, 0, 2, 3), C_h.transpose(1, 0, 2, 3), x_heads.transpose(1, 0, 2, 3))
            _, y_t = jax.lax.scan(step, h0, xs)
            y = y_t.transpose(1, 0, 2, 3)
            y = y + Dp[None, None, :, None] * x_heads
            y = y.reshape(B, T, D_INNER)
            y = _rmsnorm(y, norm_w) * jax.nn.silu(z)
            return jnp.einsum('bti,di->btd', y, out_proj_w)
        return _forward(x, in_proj_w, conv_w, conv_b, A_log, Dp, dt_bias, norm_w, out_proj_w)

    def _L0_ffn_ref(x, CB, SCB, bias):
        import jax, jax.numpy as jnp
        import numpy as np
        B, S, K, N = (8, 1024, 128, 128)
        out = jnp.einsum('bsk,nk->bsn', x, CB)
        out = out * (SCB * (1.0 / 127.0)) + bias
        return out
    x = L0_attn_x
    x = x + 0.5 * _L0_ffn_ref(_layernorm(x, axis=-1), L0_ffn_CB, L0_ffn_SCB, L0_ffn_bias)
    x = x + _L0_attn_ref(_layernorm(x, axis=-1), L0_attn_in_proj_w, L0_attn_conv_w, L0_attn_conv_b, L0_attn_A_log, L0_attn_Dp, L0_attn_dt_bias, L0_attn_norm_w, L0_attn_out_proj_w)
    x = x + 0.5 * _L0_ffn_ref(_layernorm(x, axis=-1), L0_ffn_CB, L0_ffn_SCB, L0_ffn_bias)
    return x

_drawn_inputs = setup_inputs


def setup_inputs(seed=0):
    import zlib

    import numpy as np

    out = dict(_drawn_inputs(seed))
    spreads = {'L0_attn_Dp': (1.0, 0.6), 'L0_attn_norm_w': (1.0, 0.2)}
    factors = {'L0_attn_conv_b': 8.0,
     'L0_attn_A_log': 5.166,
     'L0_attn_dt_bias': 6.454,
     'L0_ffn_bias': 8.0}
    for name, (base, spread) in spreads.items():
        noise = np.random.default_rng([zlib.crc32(name.encode()), seed]).standard_normal(out[name].shape)
        drawn = base * np.exp(spread * noise) if base else spread * noise
        out[name] = jnp.asarray(drawn.astype(out[name].dtype))
    for name, factor in factors.items():
        out[name] = (out[name] * factor).astype(out[name].dtype)
    return out
```

```python
from contextlib import ExitStack

import numpy as np

import concourse.bass as bass
from concourse import mybir

F32 = mybir.dt.float32
BF16 = mybir.dt.bfloat16
I32 = mybir.dt.int32
ALU = mybir.AluOpType
ACT = mybir.ActivationFunctionType
AX_X = mybir.AxisListType.X

EXP_LN = "natural_log_exp_and_others"
P = 128
NB = 8
NBLK = 4
T = NBLK * P
Q = 4
QT = P // Q
H = 32
HD = 8
DI = H * HD
M2 = DI // P
SLOTS = 3
LAGS = 3
TAPS = 4
EPS = 1e-5
LIMIT = 120.0
CLAMP = LIMIT / 2


def tables(general):
    k = np.arange(P)[:, None]
    s = np.arange(P)[None, :]
    i = np.arange(Q)[None, :]
    ref = (k < QT * i) + (0.0 if general else 0.5) * (k // QT == i)
    upto = k <= s
    cols = [ref[:, q:q + 1] - upto for q in range(Q)]
    cols += [k > s, np.ones((P, P))]
    cols += [upto - ref[:, np.arange(P) // QT]]
    cols += [upto]
    cols += [(k // QT < s // QT) if general else upto]
    return np.concatenate([np.asarray(c, np.float32) for c in cols], axis=1)


NSUM = Q + 4
NTAB = (NSUM + 1) * P


def build(nc, x, w_in_t, w_ffn_t, w_out_t, rows, cols, tabs, eye, place, out):
    with ExitStack() as ctx:
        def sb(name, *shape, dt=F32):
            return ctx.enter_context(nc.sbuf_tensor(name, [P, *shape], dt))

        def sem(name):
            return ctx.enter_context(nc.semaphore(name))

        bank = [ctx.enter_context(nc.psum_tensor(f"bank{i}", [P, T], F32)) for i in range(8)]

        tab = sb("tab", NTAB)
        sums = sb("sums", NSUM, P, dt=BF16)
        ident = sb("ident", P)
        w_in = sb("w_in", 2 * DI + 2 * P + H)
        w_ffn = sb("w_ffn", P)
        w_out = sb("w_out", M2, P)
        row = sb("row", 2 * P + 2 * H + DI)
        col = sb("col", M2, 8)
        scaled_ffn = sb("scaled_ffn", P)
        scaled_out = sb("scaled_out", M2, P)
        half_bias = sb("half_bias", P)
        pos_a = sb("pos_a", H)
        neg_a = sb("neg_a", H)
        eps = sb("eps", 1)
        ones = sb("ones", 1)
        worst = sb("worst", 1)

        x_in = sb("x_in", SLOTS, NBLK, P)
        stats = sb("stats", 3, NBLK, 6)
        pair = sb("pair", 3, NBLK, 4)
        mv = sb("mv", 3, NBLK, 2)
        lnv = sb("lnv", 3, NBLK)
        rstd = sb("rstd", 3, NBLK)
        xn = sb("xn", 3, NBLK, P)
        xnT = sb("xnT", 3, T)
        xb = sb("xb", NBLK, P)
        h1 = sb("h1", SLOTS, NBLK, P)
        h2 = sb("h2", NBLK, P)
        h2b = sb("h2b", NBLK, P)
        y_out = sb("y_out", SLOTS, NBLK, P)
        BT = sb("BT", SLOTS, T)
        CT = sb("CT", SLOTS, T)
        xc = sb("xc", M2, T)
        xT = sb("xT", SLOTS, M2, T)
        sz = sb("sz", SLOTS, NBLK, DI)
        dtv = sb("dtv", 4, NBLK * H)
        dt = sb("dt", SLOTS, NBLK * H)
        a = sb("a", SLOTS, NBLK * H)
        a_rest = sb("a_rest", 2, NBLK * H)
        a3 = sb("a3", SLOTS, 3, NBLK * H, dt=BF16)
        Gm = sb("Gm", NBLK, P)
        Btm = sb("Btm", NBLK - 1, P)
        Xtm = sb("Xtm", NBLK, DI)
        Dc = sb("Dc", Q, NBLK * H)
        Ed = sb("Ed", Q, NBLK * H)
        Wt = sb("Wt", Q + 1, NBLK, H)
        blk_min = sb("blk_min", 1)
        Eb = sb("Eb", SLOTS, 4, NBLK, H)
        XD = sb("XD", SLOTS, NBLK, DI)
        Xs = sb("Xs", Q + 1, NBLK, DI)
        St = sb("St", NBLK - 1, DI)
        Sd = sb("Sd", 2, DI)
        Tm = sb("Tm", NBLK, DI)
        TD = sb("TD", NBLK, DI)
        V = sb("V", NBLK, DI)
        y = sb("y", NBLK, DI)
        sq = sb("sq", NBLK, DI)
        ssq = sb("ssq", NBLK)
        yg = sb("yg", NBLK, DI)
        ygT = sb("ygT", M2, T)
        lny = sb("lny", NBLK)
        ry = sb("ry", NBLK)

        place_row = sb("place_row", T)
        distance = sb("distance", 1)
        b_pad = sb("b_pad", QT + T)
        cum_pad = sb("cum_pad", M2, QT + T)
        xdt_pad = sb("xdt_pad", M2, QT + T)
        pair_bc = h2[:].rearrange("p j d -> p (j d)")
        near_d = yg[:].rearrange("p j c -> p (j c)").rearrange("p (m t) -> p m t", m=M2)
        near_e = sq[:].rearrange("p j c -> p (j c)").rearrange("p (m t) -> p m t", m=M2)
        near_y = ygT
        low = sb("low", 1)
        flag = sb("flag", 1, dt=I32)

        MASK = tab[:, NSUM * P:]
        w_B, w_C = w_in[:, DI:DI + P], w_in[:, DI + P:DI + 2 * P]
        w_z_dt = w_in[:, DI + 2 * P:]

        s_w = sem("weights_loaded")
        s_x = [sem(f"x_loaded{i}") for i in range(SLOTS)]
        s_pa = sem("pos_a_ready")
        s_wr = sem("weights_ready")
        s_st = [sem(f"ln{i}_partial") for i in range(3)]
        s_mv = [sem(f"ln{i}_meanvar") for i in range(3)]
        s_lv = [sem(f"ln{i}_logvar") for i in range(3)]
        s_rs = [sem(f"ln{i}_rstd") for i in range(3)]
        s_nm = [sem(f"ln{i}_normed") for i in range(3)]
        s_tr = [sem(f"ln{i}_turned") for i in range(3)]
        s_ev = [sem(f"ln{i}_copied") for i in range(3)]
        s_f1 = sem("ffn1_product")
        s_xb = sem("x_plus_bias")
        s_h1 = sem("h1_ready")
        s_bc = sem("BC_product")
        s_bce = sem("BC_ready")
        s_px = sem("x_product")
        s_c0 = sem("conv_first_tap")
        s_cv = sem("conv_taps")
        s_sx = sem("xT_ready")
        s_pz = sem("z_product")
        s_sz = sem("silu_z_ready")
        s_pdt = sem("dt_product")
        s_v = sem("dt_biased")
        s_sp = sem("softplus_steps")
        s_dt = sem("dt_ready")
        s_a = sem("a_ready")
        s_a3 = sem("a_parts_ready")
        s_G = sem("G_product")
        s_gm = sem("G_masked")
        s_bt = sem("B_turned")
        s_bte = sem("B_tokens_ready")
        s_bx = sem("X_turned")
        s_bxe = sem("X_tokens_ready")
        s_D = sem("decay_sums")
        s_cl = sem("decay_clamped")
        s_red = sem("quarter_decay_read")
        s_wst = sem("worst_updated")
        s_eD = sem("source_decay_ready")
        s_eT = sem("block_decay_ready")
        s_wt = sem("source_weights_ready")
        s_xe = sem("X_to_block_end_ready")
        s_xp = sem("X_quarters_pool_ready")
        s_xd = sem("X_quarters_dve_ready")
        s_S = sem("S_product")
        s_H = sem("state_steps")
        s_Z1 = sem("Z1_product")
        s_Z2 = sem("Z2_product")
        s_y = sem("y_steps")
        s_T = sem("carried_ready")
        s_XD = sem("XD_ready")
        s_TD = sem("carried_and_skip_ready")
        s_yr = sem("y_ready")
        s_sq = sem("y_squares_summed")
        s_yg = sem("gated_ready")
        s_yt = sem("gated_turned")
        s_yte = sem("gated_copied")
        s_lry = sem("y_logms")
        s_ry = sem("y_rstd")
        s_po = sem("out_product")
        s_h2 = sem("h2_ready")
        s_h2b = sem("h2_plus_bias")
        s_f2 = sem("ffn2_product")
        s_yo = sem("y_out_ready")
        s_wt1 = sem("worst_turned")
        s_low = sem("flag_steps")
        s_flag = sem("flag_ready")
        s_gt = sem("general_tables_ready")
        s_rep = sem("near_spread")
        s_nt = sem("near_turned")
        s_nin = sem("near_inputs_copied")
        s_nd = sem("near_steps")
        s_ng = sem("near_BC_product")
        s_ne = sem("near_decay")
        s_ny = sem("near_sum_turned")
        s_near = sem("near_added")
        s_out = [sem(f"stored{i}") for i in range(SLOTS)]

        x_d = x.rearrange("b (j p) d -> b p j d", p=P)
        out_d = out.rearrange("b (j p) d -> b p j d", p=P)

        class Row:

            def __init__(self, n, k, slot, d):
                self.n, self.k, self.s, self.d = n, k, slot, d

        def row_of(n):
            return Row(n, n // SLOTS, n % SLOTS, n) if 0 <= n < NB else None

        def wait(eng, sm, value):
            if not (isinstance(value, int) and value <= 0):
                eng.wait_ge(sm, value)

        def step(stages, rows_by_lag):
            for stage, lag in stages:
                if rows_by_lag[lag] is not None:
                    stage(rows_by_lag[lag])

        def run(eng, stages):
            for n in range(LAGS - 1):
                step(stages, [row_of(n - g) for g in range(LAGS)])
            with eng.Fori(0, (NB - LAGS + 1) // SLOTS) as it:
                for u in range(SLOTS):
                    rows_by_lag = []
                    for g in range(LAGS):
                        c = LAGS - 1 + u - g
                        n = it * SLOTS + c
                        rows_by_lag.append(Row(n, it + c // SLOTS, c % SLOTS, n))
                    step(stages, rows_by_lag)
            for n in range(NB, NB + LAGS - 1):
                step(stages, [row_of(n - g) for g in range(LAGS)])

        def run_again(eng, stages, near, before=None, after=None):
            eng.wait_ge(s_flag, 1)
            needed = eng.value_load(flag[0:1, 0:1], min_val=0, max_val=1)
            with eng.If(needed > 0):
                if before is not None:
                    before()
                with eng.Fori(0, NB) as it:
                    r = Row(it + NB, it + len(range(0, NB, SLOTS)), 0, it)
                    for lag in range(LAGS):
                        if lag == LAGS - 1 and near is not None:
                            near(r)
                        for stage, g in stages:
                            if g == lag:
                                stage(r)
                if after is not None:
                    after()

        def scale_x(eng, r, qs, nq, j):
            return eng.tensor_tensor(Xs[:, qs, j, :].rearrange("p q (h e) -> p q h e", e=HD),
                                     Xtm[:, j, :].rearrange("p (h e) -> p h e", e=HD).unsqueeze(1).to_broadcast([P, nq, H, HD]),
                                     Wt[:, qs, j, :].unsqueeze(3).to_broadcast([P, nq, H, HD]), ALU.mult)

        block = ctx.enter_context(nc.Block())

        @block.sync
        def _(sp):
            def load(n):
                if n >= SLOTS:
                    sp.wait_ge(s_nm[0], n - SLOTS + 1)
                    sp.wait_ge(s_xb, n - SLOTS + 1)
                sp.dma_start(x_in[:, n % SLOTS], x_d[n]).then_inc(s_x[n % SLOTS], 16)

            for s in range(SLOTS):
                sp.sem_inc(s_out[s], 16)
            load(0)
            sp.dma_start(w_ffn[:], w_ffn_t).then_inc(s_w, 16)
            sp.dma_start(row[:], rows.partition_broadcast(P)).then_inc(s_w, 16)
            sp.dma_start(ident[:], eye).then_inc(s_w, 16)
            sp.dma_start(w_in[:], w_in_t).then_inc(s_w, 16)
            sp.dma_start(col[:], cols).then_inc(s_w, 16)
            sp.dma_start(tab[:], tabs[0]).then_inc(s_w, 16)
            sp.dma_start(w_out[:], w_out_t).then_inc(s_w, 16)

            for n in range(1, SLOTS):
                load(n)
            for n in range(NB):
                if n + SLOTS < NB:
                    load(n + SLOTS)
                sp.wait_ge(s_yo, n + 2)
                sp.dma_start(out_d[n], y_out[:, n % SLOTS]).then_inc(s_out[n % SLOTS], 16)

            def general_tables():
                sp.dma_start(tab[:], tabs[1]).then_inc(s_w, 16)
                sp.dma_start(place_row[:], place.partition_broadcast(P)).then_inc(s_w, 16)

            def load_row(r):
                sp.wait_ge(s_nm[0], r.n)
                sp.wait_ge(s_xb, r.n)
                sp.wait_ge(s_out[0], (r.k + 1) * 16)
                sp.dma_start(x_in[:, 0], x_d[bass.ds(r.d, 1)].rearrange("o p j d -> p (o j) d")).then_inc(s_x[0], 16)

            def store_row(r):
                sp.wait_ge(s_yo, r.n + 2)
                sp.dma_start(out_d[bass.ds(r.d, 1)].rearrange("o p j d -> p (o j) d"), y_out[:, 0]).then_inc(s_out[0], 16)

            for s in range(SLOTS):
                sp.wait_ge(s_out[s], 16 * (len(range(s, NB, SLOTS)) + 1))
            run_again(sp, [(load_row, 0), (store_row, 2)], None, general_tables,
                      lambda: sp.wait_ge(s_out[0], 16 * (len(range(0, NB, SLOTS)) + 1 + NB)))

        @block.tensor
        def _(pe):
            def turn(L, out_bank):
                for j in range(NBLK):
                    last = nc.tensor.transpose(out_bank[:, j * P:(j + 1) * P], xn[:, L, j, :], ident[:])
                last.then_inc(s_tr[L], 1)

            def ffn(L, out_bank, done):
                for j in range(NBLK):
                    last = nc.tensor.matmul(out_bank[:, j * P:(j + 1) * P], xnT[:, L, j * P:(j + 1) * P],
                                            scaled_ffn[:], start=True, stop=True)
                last.then_inc(done, 1)

            def ln1(r):
                wait(pe, s_v, r.n * NBLK)
                wait(pe, s_sz, r.n * NBLK)
                pe.wait_ge(s_nm[0], r.n + 1)
                turn(0, bank[0])

            def ffn1(r):
                wait(pe, s_sz, r.n * NBLK)
                pe.wait_ge(s_ev[0], r.n + 1)
                ffn(0, bank[1], s_f1)

            def ln2(r):
                pe.wait_ge(s_nm[1], r.n + 1)
                turn(1, bank[0])

            def inproj(r):
                pe.wait_ge(s_ev[1], r.n + 1)
                src = xnT[:, 1, :]
                nc.tensor.matmul(bank[0][:], w_B, src, start=True, stop=True).then_inc(s_bc, 1)
                nc.tensor.matmul(bank[1][:], w_C, src, start=True, stop=True).then_inc(s_bc, 1)
                nc.tensor.matmul(bank[2][:], w_in[:, 0:P], src, start=True, stop=True).then_inc(s_px, 1)
                pe.wait_ge(s_bce, r.n * 2 + 1)
                nc.tensor.matmul(bank[0][:], w_in[:, P:2 * P], src, start=True, stop=True).then_inc(s_px, 1)

            def z_and_dt(r):
                src = xnT[:, 1, :]
                for j in range(NBLK):
                    if j == 0:
                        pe.wait_ge(s_bce, r.n * 2 + 2)
                    elif j < 3:
                        pe.wait_ge(s_cv, r.n * 6 + 4 + j)
                    else:
                        pe.wait_ge(s_sz, r.n * NBLK + 1)
                        pe.wait_ge(s_v, r.n * NBLK + 1)
                    nc.tensor.matmul(bank[(1, 2, 0, 1)[j]][:, 0:DI + H], src[:, j * P:(j + 1) * P], w_z_dt,
                                     start=True, stop=True).then_inc(s_pz, 1)

            def prep(r):
                wait(pe, s_H, r.n * 5)
                pe.wait_ge(s_bce, r.n * 2 + 2)
                for j in range(NBLK):
                    sl = slice(j * P, (j + 1) * P)
                    last = nc.tensor.matmul(bank[3][:, sl], BT[:, r.s, sl], CT[:, r.s, sl], start=True, stop=True)
                last.then_inc(s_G, 1)
                for j in range(NBLK - 1):
                    last = nc.tensor.transpose(bank[4][:, j * P:(j + 1) * P], BT[:, r.s, j * P:(j + 1) * P], ident[:])
                last.then_inc(s_bt, 1)
                pe.wait_ge(s_sx, r.n + 1)
                for j in range(NBLK):
                    if j == 0:
                        pe.wait_ge(s_gm, r.n + 1)
                    if j == 2:
                        pe.wait_ge(s_bte, r.n + 1)
                    for m in range(M2):
                        c = (j % 2) * DI + m * P
                        last = nc.tensor.transpose(bank[3 + j // 2][:, c:c + P], xT[:, r.s, m, j * P:(j + 1) * P],
                                                   ident[:])
                    if j % 2:
                        last.then_inc(s_bx, 1)

            def decay(r):
                pe.wait_ge(s_a3, r.n + 1)
                for g in range(2):
                    pe.wait_ge(s_bxe, r.n * 2 + g + 1)
                    for i in range(4):
                        for part in range(3):
                            last = nc.tensor.matmul(bank[3 + g][:, i * P:(i + 1) * P], sums[:, 4 * g + i, :],
                                                    a3[:, r.s, part, :], start=(part == 0), stop=(part == 2))
                    last.then_inc(s_D, 1)

            def state(r):
                pe.wait_ge(s_xe, r.n + 1)
                pe.wait_ge(s_cl, r.n + 1)
                pe.wait_ge(s_eT, r.n + 1)
                for j, (bk, c) in enumerate(((3, 0), (3, DI), (4, 0))):
                    last = nc.tensor.matmul(bank[bk][:, c:c + DI], Btm[:, j, :], Xs[:, Q, j, :], start=True, stop=True)
                last.then_inc(s_S, 1)

            def mix(r):
                pe.wait_ge(s_yo, r.n + 1)
                pe.wait_ge(s_H, r.n * 5 + 5)
                for j in range(1, NBLK):
                    if j == NBLK - 1:
                        pe.wait_ge(s_T, r.n * 2 + 1)
                    c = (j - 1) % 2 * DI
                    last = nc.tensor.matmul(bank[7][:, c:c + DI], CT[:, r.s, j * P:(j + 1) * P], St[:, j - 1, :],
                                            start=True, stop=True)
                    if j != 1:
                        last.then_inc(s_Z2, 1)
                    if j == 2:
                        pe.wait_ge(s_xd, r.n + 1)
                        pe.wait_ge(s_xp, r.n + 1)
                        for i in range(NBLK):
                            for q in range(Q):
                                c = i % 2 * DI
                                last = nc.tensor.matmul(bank[5 + i // 2][q * QT:(q + 1) * QT, c:c + DI],
                                                        Gm[:, i, q * QT:(q + 1) * QT], Xs[:, q, i, :],
                                                        start=True, stop=True)
                            if i % 2:
                                last.then_inc(s_Z1, 1)

            def outproj(r):
                pe.wait_ge(s_yg, r.n + 1)
                for m in range(M2):
                    for j in range(NBLK):
                        last = nc.tensor.transpose(bank[5 + m][:, j * P:(j + 1) * P], yg[:, j, m * P:(m + 1) * P],
                                                   ident[:])
                    last.then_inc(s_yt, 1)
                pe.wait_ge(s_yte, r.n * 2 + 2)
                for j in range(NBLK):
                    for m in range(M2):
                        last = nc.tensor.matmul(bank[7][:, j * P:(j + 1) * P], ygT[:, m, j * P:(j + 1) * P],
                                                scaled_out[:, m, :], start=(m == 0), stop=(m == M2 - 1))
                last.then_inc(s_po, 1)

            def ln3(r):
                pe.wait_ge(s_nm[2], r.n + 1)
                turn(2, bank[6])

            def ffn2(r):
                pe.wait_ge(s_ev[2], r.n + 1)
                ffn(2, bank[5], s_f2)

            pe.wait_ge(s_wr, 6)
            def near(r):
                it = r.n - NB
                pe.wait_ge(s_rep, it + 1)
                for m in range(M2):
                    for j in range(NBLK):
                        last = nc.tensor.transpose(bank[5 + m][:, j * P:(j + 1) * P], V[:, j, m * P:(m + 1) * P], ident[:])
                last.then_inc(s_nt, 1)
                pe.wait_ge(s_nin, it * 2 + 1)
                for m in range(M2):
                    for j in range(NBLK):
                        last = nc.tensor.matmul(bank[5 + m][:, j * P:(j + 1) * P], y[:, j, m * P:(m + 1) * P],
                                                tab[:, (Q + 2) * P:(Q + 3) * P], start=True, stop=True)
                last.then_inc(s_nt, 1)
                with pe.Fori(0, QT) as d:
                    c = it * QT + d
                    pe.wait_ge(s_nd, c * 7 + 1)
                    nc.tensor.matmul(bank[7][:], tab[:, (Q + 1) * P:(Q + 2) * P], pair_bc[:], start=True,
                                     stop=True).then_inc(s_ng, 1)
                pe.wait_ge(s_nin, it * 2 + 2)
                pe.wait_ge(s_nd, (it + 1) * (QT * 7))
                for j in range(NBLK):
                    for m in range(M2):
                        c = j % 2 * DI + m * P
                        last = nc.tensor.transpose(bank[5 + j // 2][:, c:c + P], near_y[:, m, j * P:(j + 1) * P], ident[:])
                last.then_inc(s_ny, 1)

            stages = [(mix, 2), (prep, 1), (decay, 1), (ln1, 0), (outproj, 2), (ffn1, 0), (state, 1), (ln2, 0),
                     (ln3, 2), (inproj, 0), (ffn2, 2), (z_and_dt, 0)]
            run(pe, stages)
            pe.wait_ge(s_wst, NB)
            pe.wait_ge(s_yo, NB + 1)
            nc.tensor.matmul(bank[0][0:1, 0:P], worst[:], ident[:], start=True, stop=True).then_inc(s_wt1, 1)
            run_again(pe, stages, near, lambda: pe.wait_ge(s_gt, 1))

        @block.scalar
        def _(act):
            def rsqrt(L):
                def f(r):
                    act.wait_ge(s_mv[L], r.n + 1)
                    nc.scalar.activation(lnv[:, L, :], mv[:, L, :, 1], ACT.Ln, bias=eps[:]).then_inc(s_lv[L], 1)
                    act.wait_ge(s_lv[L], r.n + 1)
                    nc.scalar.activation(rstd[:, L, :], lnv[:, L, :], ACT.Exp, scale=-0.5).then_inc(s_rs[L], 1)
                return f

            def copy_turned(L, bk):
                def f(r):
                    act.wait_ge(s_tr[L], r.n + 1)
                    nc.scalar.copy(xnT[:, L, :], bank[bk][:]).then_inc(s_ev[L], 1)
                return f

            def inproj(r):
                act.wait_ge(s_bc, r.n * 2 + 1)
                nc.scalar.copy(BT[:, r.s, :], bank[0][:]).then_inc(s_bce, 1)
                act.wait_ge(s_bc, r.n * 2 + 2)
                nc.scalar.copy(CT[:, r.s, :], bank[1][:]).then_inc(s_bce, 1)
                for m, bk in enumerate((2, 0)):
                    act.wait_ge(s_px, r.n * 2 + m + 1)
                    nc.scalar.activation(xc[:, m, :], bank[bk][:], ACT.Identity, scale=col[:, m, TAPS - 1:TAPS],
                                         bias=col[:, m, TAPS:TAPS + 1]).then_inc(s_c0, 1)

            def silus(r):
                for m in range(M2):
                    act.wait_ge(s_cv, r.n * 6 + 5 + m)
                    last = nc.scalar.activation(xT[:, r.s, m, :], xc[:, m, :], ACT.Silu)
                last.then_inc(s_sx, 1)
                for j in range(NBLK):
                    act.wait_ge(s_pz, r.n * NBLK + j + 1)
                    nc.scalar.activation(sz[:, r.s, j, :], bank[(1, 2, 0, 1)[j]][:, 0:DI], ACT.Silu).then_inc(s_sz, 1)
                nc.scalar.preload_act_table_set(EXP_LN)

            def softplus(r):
                act.wait_ge(s_v, r.n * NBLK + NBLK)
                nc.scalar.activation(dtv[:, 1, :], dtv[:, 0, :], ACT.Abs).then_inc(s_sp, 1)
                act.wait_ge(s_sp, r.n * 3 + 1)
                nc.scalar.activation(dtv[:, 2, :], dtv[:, 1, :], ACT.Exp, scale=-1.0).then_inc(s_sp, 1)
                act.wait_ge(s_sp, r.n * 3 + 2)
                nc.scalar.activation(dtv[:, 3, :], dtv[:, 2, :], ACT.Ln, bias=ones[:]).then_inc(s_sp, 1)

            def prep(r):
                act.wait_ge(s_bt, r.n + 1)
                nc.scalar.copy(Btm[:], bank[4][:, 0:(NBLK - 1) * P].rearrange("p (j n) -> p j n", n=P)).then_inc(s_bte, 1)
                for i in range(2):
                    act.wait_ge(s_bx, r.n * 2 + i + 1)
                    nc.scalar.copy(Xtm[:, 2 * i:2 * i + 2, :],
                                   bank[3 + i][:].rearrange("p (j c) -> p j c", c=DI)).then_inc(s_bxe, 1)

            def decay(r):
                act.wait_ge(s_cl, r.n + 1)
                nc.scalar.activation(Ed[:], Dc[:], ACT.Exp).then_inc(s_eD, 1)
                act.wait_ge(s_red, r.n + 1)
                nc.scalar.activation(Eb[:, r.s].rearrange("p i j h -> p (i j h)"), bank[4][:], ACT.Exp).then_inc(s_eT, 1)

            def squares(r):
                for j in range(NBLK):
                    act.wait_ge(s_yr, r.n * 2 + j // 2 + 1)
                    last = nc.scalar.activation(sq[:, j, :], y[:, j, :], ACT.Square, accum_out=ssq[:, j:j + 1])
                last.then_inc(s_sq, 1)

            def copy_gated(r):
                for m in range(M2):
                    act.wait_ge(s_yt, r.n * 2 + m + 1)
                    nc.scalar.copy(ygT[:, m, :], bank[5 + m][:]).then_inc(s_yte, 1)

            def rms(r):
                act.wait_ge(s_sq, r.n + 1)
                nc.scalar.activation(lny[:], ssq[:], ACT.Ln, scale=1.0 / DI, bias=eps[:]).then_inc(s_lry, 1)
                act.wait_ge(s_lry, r.n + 1)
                nc.scalar.activation(ry[:], lny[:], ACT.Exp, scale=-0.5).then_inc(s_ry, 1)

            nc.scalar.preload_act_table_set(EXP_LN)
            act.wait_ge(s_w, 16 * 7)
            nc.scalar.activation(pos_a[:], row[:, 2 * P:2 * P + H], ACT.Exp).then_inc(s_pa, 1)
            act.wait_ge(s_wr, 6)
            def near(r):
                with act.Fori(0, QT) as d:
                    c = (r.n - NB) * QT + d
                    act.wait_ge(s_nd, c * 7 + 3)
                    nc.scalar.activation(near_e[:], near_d[:], ACT.Exp).then_inc(s_ne, 1)

            stages = [(squares, 2), (rms, 2), (prep, 1), (rsqrt(0), 0), (copy_gated, 2), (decay, 1),
                      (copy_turned(0, 0), 0), (rsqrt(1), 0), (rsqrt(2), 2), (copy_turned(1, 0), 0),
                      (copy_turned(2, 6), 2), (inproj, 0), (silus, 0), (softplus, 0)]
            run(act, stages)
            run_again(act, stages, near)

        @block.vector
        def _(dve):
            def meanvar(L, src, r):
                for j in range(NBLK):
                    last = nc.vector.bn_stats(stats[:, L, j, :], src[:, j, :])
                last.then_inc(s_st[L], 1)
                dve.wait_ge(s_st[L], r.n * 3 + 1)
                nc.vector.tensor_tensor(pair[:, L, :, 0:2], stats[:, L, :, 1:3], stats[:, L, :, 4:6], ALU.add)
                nc.vector.tensor_tensor(pair[:, L, :, 2], stats[:, L, :, 1], stats[:, L, :, 4],
                                        ALU.subtract).then_inc(s_st[L], 1)
                dve.wait_ge(s_st[L], r.n * 3 + 2)
                nc.vector.scalar_tensor_tensor(out=pair[:, L, :, 3], in0=pair[:, L, :, 2], scalar=0.25,
                                               in1=pair[:, L, :, 2], op0=ALU.mult, op1=ALU.mult)
                nc.vector.tensor_scalar(mv[:, L, :, 0], pair[:, L, :, 0], 0.5, None, ALU.mult).then_inc(s_st[L], 1)
                dve.wait_ge(s_st[L], r.n * 3 + 3)
                nc.vector.scalar_tensor_tensor(out=mv[:, L, :, 1], in0=pair[:, L, :, 1], scalar=1.0 / P,
                                               in1=pair[:, L, :, 3], op0=ALU.mult, op1=ALU.add).then_inc(s_mv[L], 1)

            def normalise(L, src, r):
                dve.wait_ge(s_rs[L], r.n + 1)
                for j in range(NBLK):
                    last = nc.vector.tensor_scalar(xn[:, L, j, :], src[:, j, :], mv[:, L, j, 0:1], rstd[:, L, j:j + 1],
                                                   ALU.subtract, ALU.mult)
                last.then_inc(s_nm[L], 1)

            def ln1_stats(r):
                dve.wait_ge(s_x[r.s], (r.k + 1) * 16)
                meanvar(0, x_in[:, r.s], r)

            def ln1_norm(r):
                normalise(0, x_in[:, r.s], r)

            def ffn1(r):
                dve.wait_ge(s_f1, r.n + 1)
                dve.wait_ge(s_xb, r.n + 1)
                nc.vector.tensor_tensor(h1[:, r.s], bank[1][:].rearrange("p (j d) -> p j d", d=P), xb[:],
                                        ALU.add).then_inc(s_h1, 1)
                dve.wait_ge(s_h1, r.n + 1)
                meanvar(1, h1[:, r.s], r)

            def ln2_norm(r):
                normalise(1, h1[:, r.s], r)

            def conv(r):
                for k in range(1, TAPS):
                    for m in range(M2):
                        if k == 1:
                            dve.wait_ge(s_c0, r.n * 2 + m + 1)
                        else:
                            dve.wait_ge(s_cv, r.n * 6 + (k - 2) * 2 + m + 1)
                        nc.vector.scalar_tensor_tensor(
                            out=xc[:, m, k:T], in0=bank[(2, 0)[m]][:, 0:T - k], scalar=col[:, m, TAPS - 1 - k:TAPS - k],
                            in1=xc[:, m, k:T], op0=ALU.mult, op1=ALU.add).then_inc(s_cv, 1)

            def dt_bias(r):
                for j in range(NBLK):
                    dve.wait_ge(s_pz, r.n * NBLK + j + 1)
                    dve.wait_ge(s_sz, r.n * NBLK + j + 1)
                    nc.vector.tensor_tensor(dtv[:, 0, j * H:(j + 1) * H], bank[(1, 2, 0, 1)[j]][:, DI:DI + H],
                                            row[:, 2 * P + H:2 * P + 2 * H], ALU.add).then_inc(s_v, 1)

            def dt_end(r):
                dve.wait_ge(s_sp, r.n * 3 + 3)
                nc.vector.scalar_tensor_tensor(out=dt[:, r.s, :], in0=dtv[:, 0, :], scalar=0.0, in1=dtv[:, 3, :],
                                               op0=ALU.max, op1=ALU.add).then_inc(s_dt, 1)
                dve.wait_ge(s_dt, r.n + 1)
                av = a[:, r.s, :]
                nc.vector.tensor_tensor(av.rearrange("p (j h) -> p j h", h=H),
                                        dt[:, r.s, :].rearrange("p (j h) -> p j h", h=H),
                                        neg_a[:].unsqueeze(1).to_broadcast([P, NBLK, H]), ALU.mult).then_inc(s_a, 1)
                dve.wait_ge(s_a, r.n * 5 + 1)
                nc.vector.tensor_copy(a3[:, r.s, 0, :], av).then_inc(s_a, 1)
                dve.wait_ge(s_a, r.n * 5 + 2)
                nc.vector.tensor_tensor(a_rest[:, 0, :], av, a3[:, r.s, 0, :], ALU.subtract).then_inc(s_a, 1)
                dve.wait_ge(s_a, r.n * 5 + 3)
                nc.vector.tensor_copy(a3[:, r.s, 1, :], a_rest[:, 0, :]).then_inc(s_a, 1)
                dve.wait_ge(s_a, r.n * 5 + 4)
                nc.vector.tensor_tensor(a_rest[:, 1, :], a_rest[:, 0, :], a3[:, r.s, 1, :], ALU.subtract).then_inc(s_a, 1)
                dve.wait_ge(s_a, r.n * 5 + 5)
                nc.vector.tensor_copy(a3[:, r.s, 2, :], a_rest[:, 1, :]).then_inc(s_a3, 1)

            def mask_g(r):
                dve.wait_ge(s_G, r.n + 1)
                wait(dve, s_Z1, r.n)
                nc.vector.tensor_tensor(Gm[:], bank[3][:].rearrange("p (j t) -> p j t", t=P),
                                        MASK.unsqueeze(1).to_broadcast([P, NBLK, P]), ALU.mult).then_inc(s_gm, 1)

            def clamp(r):
                dve.wait_ge(s_D, r.n * 2 + 1)
                nc.vector.tensor_scalar(Dc[:], bank[3][:].rearrange("p (q c) -> p q c", q=Q), CLAMP, None,
                                        ALU.min).then_inc(s_cl, 1)
                dve.wait_ge(s_D, r.n * 2 + 2)
                nc.vector.tensor_reduce(blk_min[:], bank[4][:, 2 * P:3 * P], AX_X, ALU.min).then_inc(s_red, 1)
                dve.wait_ge(s_red, r.n + 1)
                nc.vector.tensor_tensor(worst[:], worst[:], blk_min[:], ALU.min).then_inc(s_wst, 1)

            def weigh(r):
                dve.wait_ge(s_eD, r.n + 1)
                dve.wait_ge(s_eT, r.n + 1)
                nc.vector.tensor_tensor(Wt[:, 0:Q].rearrange("p q j h -> p q (j h)"), Ed[:],
                                        dt[:, r.s, :].unsqueeze(1).to_broadcast([P, Q, NBLK * H]), ALU.mult)
                nc.vector.tensor_tensor(Wt[:, Q].rearrange("p j h -> p (j h)"),
                                        Eb[:, r.s, 0].rearrange("p j h -> p (j h)"), dt[:, r.s, :],
                                        ALU.mult).then_inc(s_wt, 1)
                dve.wait_ge(s_bxe, r.n * 2 + 2)
                dve.wait_ge(s_wt, r.n + 1)
                for j in range(NBLK - 1):
                    last = scale_x(nc.vector, r, slice(0, Q), Q, j)
                last.then_inc(s_xd, 1)

            def states(r):
                s0, s1, s2 = bank[3][:, 0:DI], bank[3][:, DI:2 * DI], bank[4][:, 0:DI]
                dve.wait_ge(s_S, r.n + 1)

                def by_head(ap):
                    return ap.rearrange("p (h e) -> p h e", e=HD)

                def decayed(dst, src, j):
                    return nc.vector.tensor_tensor(by_head(dst), by_head(src),
                                                   Eb[:, r.s, 1, j, :].unsqueeze(2).to_broadcast([P, H, HD]), ALU.mult)
                nc.vector.tensor_copy(St[:, 0, :], s0).then_inc(s_H, 1)
                decayed(Sd[:, 0, :], s0, 1).then_inc(s_H, 1)
                dve.wait_ge(s_H, r.n * 5 + 2)
                nc.vector.tensor_tensor(St[:, 1, :], Sd[:, 0, :], s1, ALU.add).then_inc(s_H, 1)
                dve.wait_ge(s_H, r.n * 5 + 3)
                decayed(Sd[:, 1, :], St[:, 1, :], 2).then_inc(s_H, 1)
                dve.wait_ge(s_H, r.n * 5 + 4)
                nc.vector.tensor_tensor(St[:, 2, :], Sd[:, 1, :], s2, ALU.add).then_inc(s_H, 1)

            def combine(r):
                def times(out, product, i, js):
                    return nc.vector.tensor_tensor(
                        out[:, js, :].rearrange("p j (h e) -> p j h e", e=HD),
                        product.rearrange("p (j h e) -> p j h e", e=HD, h=H),
                        Eb[:, r.s, i, js, :].unsqueeze(3).to_broadcast([P, js.stop - js.start, H, HD]), ALU.mult)
                dve.wait_ge(s_Z2, r.n * 2 + 1)
                times(Tm, bank[7][:], 3, slice(1, 3)).then_inc(s_T, 1)
                for g in range(2):
                    dve.wait_ge(s_Z1, r.n * 2 + g + 1)
                    times(V, bank[5 + g][:], 2, slice(2 * g, 2 * g + 2)).then_inc(s_y, 1)
                    if g == 0:
                        dve.wait_ge(s_Z2, r.n * 2 + 2)
                        times(Tm, bank[7][:, 0:DI], 3, slice(3, 4)).then_inc(s_T, 1)
                for g in range(2):
                    js = slice(2 * g, 2 * g + 2)
                    dve.wait_ge(s_y, r.n * 2 + g + 1)
                    dve.wait_ge(s_TD, r.n * 2 + g + 1)
                    nc.vector.tensor_tensor(y[:, js, :], V[:, js, :], TD[:, js, :], ALU.add).then_inc(s_yr, 1)

            def residual2(r):
                dve.wait_ge(s_po, r.n + 1)
                dve.wait_ge(s_ry, r.n + 1)
                for j in range(NBLK):
                    last = nc.vector.scalar_tensor_tensor(out=h2[:, j, :], in0=bank[7][:, j * P:(j + 1) * P],
                                                          scalar=ry[:, j:j + 1], in1=h1[:, r.s, j, :],
                                                          op0=ALU.mult, op1=ALU.add)
                last.then_inc(s_h2, 1)
                dve.wait_ge(s_h2, r.n + 1)
                meanvar(2, h2[:], r)

            def ln3_norm(r):
                normalise(2, h2[:], r)

            def finish(r):
                dve.wait_ge(s_f2, r.n + 1)
                dve.wait_ge(s_h2b, r.n + 1)
                dve.wait_ge(s_out[r.s], (r.k + 1) * 16)
                nc.vector.tensor_tensor(y_out[:, r.s], bank[5][:].rearrange("p (j d) -> p j d", d=P), h2b[:],
                                        ALU.add).then_inc(s_yo, 1)

            nc.vector.memset(eps[:], EPS).then_inc(s_yo, 1)
            nc.vector.memset(ones[:], 1.0)
            nc.vector.memset(Tm[:, 0, :], 0.0)
            nc.vector.memset(worst[:], 0.0).then_inc(s_wr, 1)
            dve.wait_ge(s_w, 16 * 7)
            nc.vector.scalar_tensor_tensor(out=scaled_ffn[:], in0=w_ffn[:], scalar=0.5 / 127.0, in1=row[:, 0:P],
                                           op0=ALU.mult, op1=ALU.mult).then_inc(s_wr, 1)
            nc.vector.tensor_copy(sums[:], tab[:, 0:NSUM * P].rearrange("p (i s) -> p i s", s=P)).then_inc(s_wr, 1)
            nc.vector.tensor_scalar(half_bias[:], row[:, P:2 * P], 0.5, None, ALU.mult).then_inc(s_wr, 1)
            for m in range(M2):
                last = nc.vector.tensor_scalar(scaled_out[:, m, :], w_out[:, m, :], col[:, m, TAPS + 2:TAPS + 3], None,
                                               ALU.mult)
            last.then_inc(s_wr, 1)
            dve.wait_ge(s_pa, 1)
            nc.vector.tensor_scalar(neg_a[:], pos_a[:], -1.0, None, ALU.mult).then_inc(s_wr, 1)
            dve.wait_ge(s_wr, 6)
            def near(r):
                it = r.n - NB
                dve.wait_ge(s_XD, r.n + 1)
                by_head = "p j (h e) -> p j h e"

                def spread(v):
                    return v[:, r.s, :].rearrange("p (j h) -> p j h", h=H).unsqueeze(3).to_broadcast([P, NBLK, H, HD])
                nc.vector.tensor_tensor(V[:].rearrange(by_head, e=HD), Xtm[:].rearrange(by_head, e=HD), spread(dt), ALU.mult)
                nc.vector.tensor_copy(y[:].rearrange(by_head, e=HD), spread(a)).then_inc(s_rep, 1)
                nc.vector.tensor_copy(b_pad[:, QT:], BT[:, r.s, :])
                nc.vector.memset(distance[:], 0.0)
                for k, target in enumerate((xdt_pad, cum_pad)):
                    dve.wait_ge(s_nt, it * 2 + k + 1)
                    for m in range(M2):
                        last = nc.vector.tensor_copy(target[:, m, QT:], bank[5 + m][:])
                    last.then_inc(s_nin, 1)
                dve.wait_ge(s_nin, it * 2 + 2)
                nc.vector.memset(near_y[:], 0.0)
                with dve.Fori(0, QT) as d:
                    c = it * QT + d
                    back = bass.ds(QT - d, T)
                    nc.vector.tensor_tensor(pair_bc[:], CT[:, r.s, :], b_pad[:, back], ALU.mult).then_inc(s_nd, 1)
                    nc.vector.tensor_tensor(near_d[:], cum_pad[:, :, QT:], cum_pad[:, :, back], ALU.subtract).then_inc(s_nd, 1)
                    dve.wait_ge(s_nd, c * 7 + 2)
                    nc.vector.tensor_scalar(near_d[:], near_d[:], 0.0, None, ALU.min).then_inc(s_nd, 1)
                    dve.wait_ge(s_ne, c + 1)
                    nc.vector.scalar_tensor_tensor(out=near_e[:], in0=place_row[:].unsqueeze(1).to_broadcast([P, M2, T]),
                                                   scalar=distance[:], in1=near_e[:], op0=ALU.is_ge,
                                                   op1=ALU.mult).then_inc(s_nd, 1)
                    dve.wait_ge(s_nd, c * 7 + 4)
                    nc.vector.tensor_tensor(near_e[:], near_e[:], xdt_pad[:, :, back], ALU.mult).then_inc(s_nd, 1)
                    nc.vector.tensor_scalar(distance[:], distance[:], 1.0, None, ALU.add)
                    dve.wait_ge(s_nd, c * 7 + 5)
                    dve.wait_ge(s_ng, c + 1)
                    nc.vector.tensor_tensor(near_e[:], near_e[:], bank[7][:].unsqueeze(1).to_broadcast([P, M2, T]),
                                            ALU.mult).then_inc(s_nd, 1)
                    dve.wait_ge(s_nd, c * 7 + 6)
                    nc.vector.tensor_tensor(near_y[:], near_y[:], near_e[:], ALU.add).then_inc(s_nd, 1)
                    dve.wait_ge(s_nd, c * 7 + 7)
                dve.wait_ge(s_ny, it + 1)
                for g in range(2):
                    last = nc.vector.tensor_tensor(XD[:, r.s, 2 * g:2 * g + 2, :], XD[:, r.s, 2 * g:2 * g + 2, :],
                                                   bank[5 + g][:].rearrange("p (j c) -> p j c", c=DI), ALU.add)
                last.then_inc(s_near, 1)

            def general_tables():
                dve.wait_ge(s_w, 16 * 9)
                nc.vector.memset(b_pad[:, 0:QT], 0.0)
                nc.vector.memset(cum_pad[:, :, 0:QT], 0.0)
                nc.vector.memset(xdt_pad[:, :, 0:QT], 0.0)
                nc.vector.tensor_copy(sums[:], tab[:, 0:NSUM * P].rearrange("p (i s) -> p i s", s=P)).then_inc(s_gt, 1)

            stages = [(combine, 2), (mask_g, 1), (ln1_stats, 0), (clamp, 1), (ln1_norm, 0), (weigh, 1), (ffn1, 0),
                      (residual2, 2), (states, 1), (ln2_norm, 0), (ln3_norm, 2), (conv, 0), (finish, 2),
                      (dt_bias, 0), (dt_end, 0)]
            run(dve, stages)
            dve.wait_ge(s_wt1, 1)
            nc.vector.tensor_reduce(low[0:1, :], bank[0][0:1, 0:P], AX_X, ALU.min).then_inc(s_low, 1)
            dve.wait_ge(s_low, 1)
            nc.vector.tensor_scalar(flag[0:1, :], low[0:1, :], -LIMIT / 2, None, ALU.is_lt).then_inc(s_flag, 1)
            run_again(dve, stages, near, general_tables)

        @block.gpsimd
        def _(pool):
            def bias1(r):
                pool.wait_ge(s_x[r.s], (r.k + 1) * 16)
                wait(pool, s_h1, r.n)
                nc.gpsimd.tensor_tensor(xb[:], x_in[:, r.s], half_bias[:].unsqueeze(1).to_broadcast([P, NBLK, P]),
                                        ALU.add).then_inc(s_xb, 1)

            def weigh(r):
                pool.wait_ge(s_wt, r.n + 1)
                pool.wait_ge(s_bxe, r.n * 2 + 2)
                for j in range(NBLK - 1):
                    last = scale_x(nc.gpsimd, r, slice(Q, Q + 1), 1, j)
                last.then_inc(s_xe, 1)
                scale_x(nc.gpsimd, r, slice(0, Q), Q, NBLK - 1).then_inc(s_xp, 1)

            def skip(r):
                pool.wait_ge(s_bxe, r.n * 2 + 2)
                nc.gpsimd.tensor_tensor(XD[:, r.s], Xtm[:], row[:, 2 * P + 2 * H:].unsqueeze(1).to_broadcast([P, NBLK, DI]),
                                        ALU.mult).then_inc(s_XD, 1)

            def carried(r):
                pool.wait_ge(s_XD, r.n + 1)
                wait(pool, s_yr, r.n * 2)
                pool.wait_ge(s_T, r.n * 2 + 1)
                nc.gpsimd.tensor_tensor(TD[:, 0:2, :], Tm[:, 0:2, :], XD[:, r.s, 0:2, :], ALU.add).then_inc(s_TD, 1)
                pool.wait_ge(s_T, r.n * 2 + 2)
                nc.gpsimd.tensor_tensor(TD[:, 2:4, :], Tm[:, 2:4, :], XD[:, r.s, 2:4, :], ALU.add).then_inc(s_TD, 1)

            def gate(r):
                for g in range(2):
                    js = slice(2 * g, 2 * g + 2)
                    pool.wait_ge(s_yr, r.n * 2 + g + 1)
                    last = nc.gpsimd.tensor_tensor(yg[:, js, :], y[:, js, :], sz[:, r.s, js, :], ALU.mult)
                last.then_inc(s_yg, 1)

            def bias2(r):
                pool.wait_ge(s_h2, r.n + 1)
                nc.gpsimd.tensor_tensor(h2b[:], h2[:], half_bias[:].unsqueeze(1).to_broadcast([P, NBLK, P]),
                                        ALU.add).then_inc(s_h2b, 1)

            pool.wait_ge(s_wr, 6)
            def near(r):
                pool.wait_ge(s_near, r.n - NB + 1)

            stages = [(carried, 2), (gate, 2), (bias1, 0), (skip, 1), (weigh, 1), (bias2, 2)]
            run(pool, stages)
            run_again(pool, stages, near)


def kernel(L0_attn_x, L0_attn_in_proj_w, L0_attn_conv_w, L0_attn_conv_b, L0_attn_A_log, L0_attn_Dp,
           L0_attn_dt_bias, L0_attn_norm_w, L0_attn_out_proj_w, L0_ffn_CB, L0_ffn_SCB, L0_ffn_bias):
    import concourse.bacc as bacc
    from concourse.bass_utils import run_bass_kernel_spmd

    def inner(v):
        v = np.asarray(v)
        return v.reshape(M2, P, -1).transpose(1, 0, 2)

    w_in = np.asarray(L0_attn_in_proj_w).T
    filler = np.zeros((P, M2, 1), np.float32)
    arrays = {
        "x": L0_attn_x,
        "w_in_t": np.concatenate([w_in[:, :DI], w_in[:, 2 * DI:2 * DI + 2 * P], w_in[:, DI:2 * DI],
                                  w_in[:, 2 * DI + 2 * P:]], axis=1),
        "w_ffn_t": np.asarray(L0_ffn_CB).T,
        "w_out_t": inner(np.asarray(L0_attn_out_proj_w).T),
        "rows": np.concatenate([np.asarray(v) for v in (L0_ffn_SCB, L0_ffn_bias, L0_attn_A_log, L0_attn_dt_bias,
                                                        np.repeat(np.asarray(L0_attn_Dp), HD))]),
        "cols": np.concatenate([inner(L0_attn_conv_w), inner(L0_attn_conv_b), inner(np.repeat(np.asarray(L0_attn_Dp), HD)),
                                inner(L0_attn_norm_w), filler], axis=2),
        "tabs": np.stack([tables(False), tables(True)]),
        "eye": np.eye(P, dtype=np.float32),
        "place": (np.arange(T) % QT).astype(np.float32),
    }
    arrays = {k: np.ascontiguousarray(v) for k, v in arrays.items()}
    nc = bacc.Bacc("TRN2", target_bir_lowering=False, num_devices=1)
    args = [nc.dram_tensor(k, v.shape, mybir.dt.from_np(v.dtype), kind="ExternalInput").ap() for k, v in arrays.items()]
    args.append(nc.dram_tensor("out", arrays["x"].shape, F32, kind="ExternalOutput").ap())
    build(nc, *args)
    r = run_bass_kernel_spmd(nc, [arrays], core_ids=[0])
    return r.results[0]["out"]
```

```python
from contextlib import ExitStack

import numpy as np

import concourse.bass as bass
from concourse import mybir

F32 = mybir.dt.float32
BF16 = mybir.dt.bfloat16
I32 = mybir.dt.int32
ALU = mybir.AluOpType
ACT = mybir.ActivationFunctionType
AX_X = mybir.AxisListType.X

EXP_LN = "natural_log_exp_and_others"
P = 128
NB = 8
NBLK = 4
T = NBLK * P
Q = 4
QT = P // Q
H = 32
HD = 8
DI = H * HD
M2 = DI // P
SLOTS = 3
LAGS = 3
TAPS = 4
EPS = 1e-5
LIMIT = 120.0
CLAMP = LIMIT / 2


def tables(general):
    k = np.arange(P)[:, None]
    s = np.arange(P)[None, :]
    i = np.arange(Q)[None, :]
    ref = (k < QT * i) + (0.0 if general else 0.5) * (k // QT == i)
    upto = k <= s
    cols = [ref[:, q:q + 1] - upto for q in range(Q)]
    cols += [k > s, np.ones((P, P))]
    cols += [upto]
    cols += [upto - ref[:, np.arange(P) // QT]]
    cols += [(k // QT < s // QT) if general else upto]
    return np.concatenate([np.asarray(c, np.float32) for c in cols], axis=1)


NSUM = Q + 4
NTAB = (NSUM + 1) * P


def build(nc, x, w_in_t, w_ffn_t, w_out_t, rows, cols, tabs, eye, place, out):
    with ExitStack() as ctx:
        def sb(name, *shape, dt=F32):
            return ctx.enter_context(nc.sbuf_tensor(name, [P, *shape], dt))

        def sem(name):
            return ctx.enter_context(nc.semaphore(name))

        bank = [ctx.enter_context(nc.psum_tensor(f"bank{i}", [P, T], F32)) for i in range(8)]

        tab = sb("tab", NTAB)
        sums = sb("sums", NSUM, P, dt=BF16)
        ident = sb("ident", P)
        w_in = sb("w_in", 2 * DI + 2 * P + H)
        w_ffn = sb("w_ffn", P)
        w_out = sb("w_out", M2, P)
        row = sb("row", 2 * P + 2 * H + DI)
        col = sb("col", M2, TAPS + 2)
        scaled_ffn = sb("scaled_ffn", P)
        scaled_out = sb("scaled_out", M2, P)
        half_bias = sb("half_bias", P)
        pos_a = sb("pos_a", H)
        neg_a = sb("neg_a", H)
        eps = sb("eps", 1)
        ones = sb("ones", 1)
        worst = sb("worst", NBLK * H)
        lowest = sb("lowest", 1)

        x_in = sb("x_in", SLOTS, NBLK, P)
        stats = sb("stats", 3, NBLK, 6)
        pair = sb("pair", 3, NBLK, 4)
        mv = sb("mv", 3, NBLK, 2)
        lnv = sb("lnv", 3, NBLK)
        rstd = sb("rstd", 3, NBLK)
        neg_mr = sb("neg_mr", 3, NBLK)
        xn = sb("xn", 3, NBLK, P)
        xnT = sb("xnT", 3, T)
        xb = sb("xb", NBLK, P)
        h1 = sb("h1", SLOTS, NBLK, P)
        h2 = sb("h2", NBLK, P)
        h2b = sb("h2b", NBLK, P)
        y_out = sb("y_out", SLOTS, NBLK, P)
        BT = sb("BT", SLOTS, T)
        CT = sb("CT", SLOTS, T)
        xc = sb("xc", M2, T)
        xT = sb("xT", SLOTS, M2, T)
        sz = sb("sz", SLOTS, NBLK, DI)
        dtv = sb("dtv", 4, NBLK * H)
        dt = sb("dt", SLOTS, NBLK * H)
        a = sb("a", SLOTS, NBLK * H)
        a_rest = sb("a_rest", 2, NBLK * H)
        a3 = sb("a3", SLOTS, 3, NBLK * H, dt=BF16)
        Gm = sb("Gm", NBLK, P)
        Btm = sb("Btm", NBLK - 1, P)
        Xtm = sb("Xtm", NBLK, DI)
        Dc = sb("Dc", Q + 1, NBLK * H)
        Ed = sb("Ed", Q, NBLK * H)
        Wt = sb("Wt", Q + 1, NBLK, H)
        Eb = sb("Eb", SLOTS, 4, NBLK, H)
        XD = sb("XD", SLOTS, NBLK, DI)
        Xs = sb("Xs", Q + 1, NBLK, DI)
        St = sb("St", NBLK - 1, DI)
        Sd = sb("Sd", 2, DI)
        Tm = sb("Tm", NBLK, DI)
        TD = sb("TD", NBLK, DI)
        V = sb("V", NBLK, DI)
        y = sb("y", NBLK, DI)
        sq = sb("sq", NBLK, DI)
        ssq = sb("ssq", NBLK)
        yg = sb("yg", NBLK, DI)
        ygT = sb("ygT", M2, T)
        lny = sb("lny", NBLK)
        ry = sb("ry", NBLK)

        place_row = sb("place_row", T)
        distance = sb("distance", 1)
        b_pad = sb("b_pad", QT + T)
        cum_pad = sb("cum_pad", M2, QT + T)
        xdt_pad = sb("xdt_pad", M2, QT + T)
        pair_bc = h2[:].rearrange("p j d -> p (j d)")
        near_d = yg[:].rearrange("p j c -> p (j c)").rearrange("p (m t) -> p m t", m=M2)
        near_e = sq[:].rearrange("p j c -> p (j c)").rearrange("p (m t) -> p m t", m=M2)
        near_y = ygT
        low = sb("low", 1)
        flag = sb("flag", 1, dt=I32)

        MASK = tab[:, NSUM * P:]
        w_B, w_C = w_in[:, DI:DI + P], w_in[:, DI + P:DI + 2 * P]
        w_z_dt = w_in[:, DI + 2 * P:]

        s_load = {name: sem(f"{name}_loaded") for name in ("ident", "w_ffn", "row", "w_in", "col", "tab", "w_out",
                                                           "general_tab", "place")}
        s_x = [sem(f"x_loaded{i}") for i in range(SLOTS)]
        s_pa = sem("pos_a_ready")
        s_eps = sem("eps_ready")
        s_wr = sem("weights_ready")
        s_st = [sem(f"ln{i}_partial") for i in range(3)]
        s_mv = [sem(f"ln{i}_meanvar") for i in range(3)]
        s_lv = [sem(f"ln{i}_logvar") for i in range(3)]
        s_rs = [sem(f"ln{i}_rstd") for i in range(3)]
        s_nb = [sem(f"ln{i}_bias") for i in range(3)]
        s_nm = [sem(f"ln{i}_normed") for i in range(3)]
        s_nv = [sem(f"ln{i}_normed_by_dve") for i in range(3)]
        s_tr = [sem(f"ln{i}_turned") for i in range(3)]
        s_ev = [sem(f"ln{i}_copied") for i in range(3)]
        s_f1 = sem("ffn1_product")
        s_xb = sem("x_plus_bias")
        s_h1 = sem("h1_ready")
        s_bc = sem("BC_product")
        s_bce = sem("BC_ready")
        s_px = sem("x_product")
        s_c0 = sem("conv_first_tap")
        s_cv = sem("conv_taps")
        s_sx = sem("xT_ready")
        s_pz = sem("z_product")
        s_sz = sem("silu_z_ready")
        s_v = sem("dt_biased")
        s_sp = sem("softplus_steps")
        s_dt = sem("dt_ready")
        s_a = sem("a_ready")
        s_a3 = sem("a_parts_ready")
        s_ar = sem("a_rests_ready")
        s_G = sem("G_product")
        s_gm = sem("G_masked")
        s_bt = sem("B_turned")
        s_bte = sem("B_tokens_ready")
        s_bx = sem("X_turned")
        s_bxe = sem("X_tokens_ready")
        s_D = sem("decay_sums")
        s_cl = sem("decay_clamped")
        s_wst = sem("worst_updated")
        s_eD = sem("source_decay_ready")
        s_eT = sem("block_decay_ready")
        s_wt = sem("source_weights_ready")
        s_xe = sem("X_to_block_end_ready")
        s_xp = sem("X_quarters_pool_ready")
        s_xd = sem("X_quarters_dve_ready")
        s_S = sem("S_product")
        s_H = sem("state_steps")
        s_st0 = sem("first_state_ready")
        s_Z1 = sem("Z1_product")
        s_Z2 = sem("Z2_product")
        s_y = sem("y_steps")
        s_T = sem("carried_ready")
        s_XD = sem("XD_ready")
        s_TD = sem("carried_and_skip_ready")
        s_yr = sem("y_ready")
        s_sq = sem("y_squares_summed")
        s_yg = sem("gated_ready")
        s_yt = sem("gated_turned")
        s_yte = sem("gated_copied")
        s_lry = sem("y_logms")
        s_ry = sem("y_rstd")
        s_po = sem("out_product")
        s_h2 = sem("h2_ready")
        s_h2b = sem("h2_plus_bias")
        s_f2 = sem("ffn2_product")
        s_yo = sem("y_out_ready")
        s_wt1 = sem("worst_turned")
        s_low = sem("flag_steps")
        s_flag = sem("flag_ready")
        s_gt = sem("general_tables_ready")
        s_rep = sem("near_spread")
        s_nt = sem("near_turned")
        s_nin = sem("near_inputs_copied")
        s_nd = sem("near_steps")
        s_ng = sem("near_BC_product")
        s_ne = sem("near_decay")
        s_ny = sem("near_sum_turned")
        s_near = sem("near_added")
        s_out = [sem(f"stored{i}") for i in range(SLOTS)]

        x_d = x.rearrange("b (j p) d -> b p j d", p=P)
        out_d = out.rearrange("b (j p) d -> b p j d", p=P)

        class Row:

            def __init__(self, n, k, slot, d):
                self.n, self.k, self.s, self.d = n, k, slot, d

        def row_of(n):
            return Row(n, n // SLOTS, n % SLOTS, n) if 0 <= n < NB else None

        def wait(eng, sm, value):
            if not (isinstance(value, int) and value <= 0):
                eng.wait_ge(sm, value)

        def first(eng, r, sm, value=16):
            if isinstance(r.n, int) and r.n == 0:
                eng.wait_ge(sm, value)

        def step(stages, rows_by_lag):
            for stage, lag in stages:
                if rows_by_lag[lag] is not None:
                    stage(rows_by_lag[lag])

        def run(eng, stages):
            for n in range(LAGS - 1):
                step(stages, [row_of(n - g) for g in range(LAGS)])
            with eng.Fori(0, (NB - LAGS + 1) // SLOTS) as it:
                for u in range(SLOTS):
                    rows_by_lag = []
                    for g in range(LAGS):
                        c = LAGS - 1 + u - g
                        n = it * SLOTS + c
                        rows_by_lag.append(Row(n, it + c // SLOTS, c % SLOTS, n))
                    step(stages, rows_by_lag)
            for n in range(NB, NB + LAGS - 1):
                step(stages, [row_of(n - g) for g in range(LAGS)])

        def run_again(eng, by_row, before=None, after=None):
            eng.wait_ge(s_flag, 1)
            needed = eng.value_load(flag[0:1, 0:1], min_val=0, max_val=1)
            with eng.If(needed > 0):
                if before is not None:
                    before()
                with eng.Fori(0, NB) as it:
                    r = Row(it + NB, it + len(range(0, NB, SLOTS)), 0, it)
                    for stage in by_row:
                        stage(r)
                if after is not None:
                    after()

        def scale_x(eng, r, qs, nq, j):
            return eng.tensor_tensor(Xs[:, qs, j, :].rearrange("p q (h e) -> p q h e", e=HD),
                                     Xtm[:, j, :].rearrange("p (h e) -> p h e", e=HD).unsqueeze(1).to_broadcast([P, nq, H, HD]),
                                     Wt[:, qs, j, :].unsqueeze(3).to_broadcast([P, nq, H, HD]), ALU.mult)

        block = ctx.enter_context(nc.Block())

        @block.sync
        def _(sp):
            def load(n):
                if n >= SLOTS:
                    sp.wait_ge(s_nm[0], n - SLOTS + 1)
                    sp.wait_ge(s_nv[0], n - SLOTS + 1)
                    sp.wait_ge(s_xb, n - SLOTS + 1)
                sp.dma_start(x_in[:, n % SLOTS], x_d[n]).then_inc(s_x[n % SLOTS], 16)

            for s in range(SLOTS):
                sp.sem_inc(s_out[s], 16)
            sp.sem_inc(s_yo, 1)
            load(0)
            for name, buffer, source in (("ident", ident, eye), ("w_ffn", w_ffn, w_ffn_t),
                                         ("row", row, rows.partition_broadcast(P)), ("w_in", w_in, w_in_t),
                                         ("col", col, cols), ("tab", tab, tabs[0]), ("w_out", w_out, w_out_t)):
                sp.dma_start(buffer[:], source).then_inc(s_load[name], 16)

            for n in range(1, SLOTS):
                load(n)
            for n in range(NB):
                if n + SLOTS < NB:
                    load(n + SLOTS)
                sp.wait_ge(s_yo, n + 2)
                sp.dma_start(out_d[n], y_out[:, n % SLOTS]).then_inc(s_out[n % SLOTS], 16)

            def general_tables():
                sp.dma_start(tab[:], tabs[1]).then_inc(s_load["general_tab"], 16)
                sp.dma_start(place_row[:], place.partition_broadcast(P)).then_inc(s_load["place"], 16)

            def load_row(r):
                sp.wait_ge(s_nv[0], r.n)
                sp.wait_ge(s_nm[0], r.n)
                sp.wait_ge(s_xb, r.n)
                sp.wait_ge(s_out[0], (r.k + 1) * 16)
                sp.dma_start(x_in[:, 0], x_d[bass.ds(r.d, 1)].rearrange("o p j d -> p (o j) d")).then_inc(s_x[0], 16)

            def store_row(r):
                sp.wait_ge(s_yo, r.n + 2)
                sp.dma_start(out_d[bass.ds(r.d, 1)].rearrange("o p j d -> p (o j) d"), y_out[:, 0]).then_inc(s_out[0], 16)

            for s in range(SLOTS):
                sp.wait_ge(s_out[s], 16 * (len(range(s, NB, SLOTS)) + 1))
            run_again(sp, [load_row, store_row], general_tables,
                      lambda: sp.wait_ge(s_out[0], 16 * (len(range(0, NB, SLOTS)) + 1 + NB)))

        @block.tensor
        def _(pe):
            def turn(L, out_bank):
                for j in range(NBLK):
                    last = nc.tensor.transpose(out_bank[:, j * P:(j + 1) * P], xn[:, L, j, :], ident[:])
                last.then_inc(s_tr[L], 1)

            def ffn(L, out_bank, done):
                for j in range(NBLK):
                    last = nc.tensor.matmul(out_bank[:, j * P:(j + 1) * P], xnT[:, L, j * P:(j + 1) * P],
                                            scaled_ffn[:], start=True, stop=True)
                last.then_inc(done, 1)

            def ln1(r):
                first(pe, r, s_load["ident"])
                wait(pe, s_v, r.n * NBLK)
                wait(pe, s_sz, r.n * NBLK)
                pe.wait_ge(s_nm[0], r.n + 1)
                pe.wait_ge(s_nv[0], r.n + 1)
                turn(0, bank[0])

            def ffn1(r):
                first(pe, r, s_wr, 1)
                wait(pe, s_sz, r.n * NBLK)
                pe.wait_ge(s_ev[0], r.n + 1)
                ffn(0, bank[1], s_f1)

            def ln2(r):
                pe.wait_ge(s_nm[1], r.n + 1)
                pe.wait_ge(s_nv[1], r.n + 1)
                turn(1, bank[0])

            def project_bc(r):
                first(pe, r, s_load["w_in"])
                pe.wait_ge(s_ev[1], r.n + 1)
                nc.tensor.matmul(bank[0][:], w_B, xnT[:, 1, :], start=True, stop=True).then_inc(s_bc, 1)
                nc.tensor.matmul(bank[1][:], w_C, xnT[:, 1, :], start=True, stop=True).then_inc(s_bc, 1)

            def project_x(r):
                nc.tensor.matmul(bank[2][:], w_in[:, 0:P], xnT[:, 1, :], start=True, stop=True).then_inc(s_px, 1)
                pe.wait_ge(s_bce, r.n * 2 + 1)
                nc.tensor.matmul(bank[0][:], w_in[:, P:2 * P], xnT[:, 1, :], start=True, stop=True).then_inc(s_px, 1)

            def project_z_dt(j):
                def block_j(r):
                    if j == 0:
                        pe.wait_ge(s_bce, r.n * 2 + 2)
                    elif j < 3:
                        pe.wait_ge(s_cv, r.n * 6 + 4 + j)
                    else:
                        pe.wait_ge(s_sz, r.n * NBLK + 1)
                        pe.wait_ge(s_v, r.n * NBLK + 1)
                    nc.tensor.matmul(bank[(1, 2, 0, 1)[j]][:, 0:DI + H], xnT[:, 1, j * P:(j + 1) * P], w_z_dt,
                                     start=True, stop=True).then_inc(s_pz, 1)
                return block_j

            def pairs(r):
                wait(pe, s_H, r.n * 4)
                pe.wait_ge(s_bce, r.n * 2 + 2)
                for j in range(NBLK):
                    sl = slice(j * P, (j + 1) * P)
                    last = nc.tensor.matmul(bank[3][:, sl], BT[:, r.s, sl], CT[:, r.s, sl], start=True, stop=True)
                last.then_inc(s_G, 1)

            def turn_b(r):
                wait(pe, s_H, r.n * 4)
                for j in range(NBLK - 1):
                    last = nc.tensor.transpose(bank[4][:, j * P:(j + 1) * P], BT[:, r.s, j * P:(j + 1) * P], ident[:])
                last.then_inc(s_bt, 1)

            def turn_x(g):
                def half_g(r):
                    if g == 0:
                        pe.wait_ge(s_sx, r.n + 1)
                        pe.wait_ge(s_gm, r.n + 1)
                    else:
                        pe.wait_ge(s_bte, r.n + 1)
                    for j in (2 * g, 2 * g + 1):
                        for m in range(M2):
                            c = (j % 2) * DI + m * P
                            last = nc.tensor.transpose(bank[3 + g][:, c:c + P], xT[:, r.s, m, j * P:(j + 1) * P],
                                                       ident[:])
                    last.then_inc(s_bx, 1)
                return half_g

            def decay(g):
                def sums_g(r):
                    if g == 0:
                        first(pe, r, s_wr, 5)
                        pe.wait_ge(s_a3, r.n * 3 + 3)
                    pe.wait_ge(s_bxe, r.n * 2 + g + 1)
                    for i in range(4):
                        for part in range(3):
                            last = nc.tensor.matmul(bank[3 + g][:, i * P:(i + 1) * P], sums[:, 4 * g + i, :],
                                                    a3[:, r.s, part, :], start=(part == 0), stop=(part == 2))
                    last.then_inc(s_D, 1)
                return sums_g

            def state(r):
                pe.wait_ge(s_xe, r.n + 1)
                pe.wait_ge(s_cl, r.n + 1)
                pe.wait_ge(s_eT, r.n + 1)
                for j, (bk, c) in enumerate(((3, 0), (3, DI), (4, 0))):
                    last = nc.tensor.matmul(bank[bk][:, c:c + DI], Btm[:, j, :], Xs[:, Q, j, :], start=True, stop=True)
                last.then_inc(s_S, 1)

            def carry(r):
                pe.wait_ge(s_yo, r.n + 1)
                pe.wait_ge(s_H, r.n * 4 + 4)
                pe.wait_ge(s_st0, r.n + 1)
                for j in (1, 2):
                    last = nc.tensor.matmul(bank[7][:, (j - 1) * DI:j * DI], CT[:, r.s, j * P:(j + 1) * P], St[:, j - 1, :],
                                            start=True, stop=True)
                last.then_inc(s_Z2, 1)

            def carry_last(r):
                pe.wait_ge(s_T, r.n * 2 + 1)
                nc.tensor.matmul(bank[7][:, 0:DI], CT[:, r.s, 3 * P:4 * P], St[:, 2, :], start=True,
                                 stop=True).then_inc(s_Z2, 1)

            def quarters(g):
                def half_g(r):
                    if g == 0:
                        pe.wait_ge(s_xd, r.n + 1)
                        pe.wait_ge(s_xp, r.n + 1)
                    for i in (2 * g, 2 * g + 1):
                        for q in range(Q):
                            c = i % 2 * DI
                            last = nc.tensor.matmul(bank[5 + i // 2][q * QT:(q + 1) * QT, c:c + DI],
                                                    Gm[:, i, q * QT:(q + 1) * QT], Xs[:, q, i, :],
                                                    start=True, stop=True)
                    last.then_inc(s_Z1, 1)
                return half_g

            def turn_gated(r):
                pe.wait_ge(s_yg, r.n * 2 + 2)
                for m in range(M2):
                    for j in range(NBLK):
                        last = nc.tensor.transpose(bank[5 + m][:, j * P:(j + 1) * P], yg[:, j, m * P:(m + 1) * P],
                                                   ident[:])
                    last.then_inc(s_yt, 1)

            def project_out(r):
                pe.wait_ge(s_yte, r.n * 2 + 2)
                for j in range(NBLK):
                    for m in range(M2):
                        last = nc.tensor.matmul(bank[7][:, j * P:(j + 1) * P], ygT[:, m, j * P:(j + 1) * P],
                                                scaled_out[:, m, :], start=(m == 0), stop=(m == M2 - 1))
                last.then_inc(s_po, 1)

            def ln3(r):
                pe.wait_ge(s_nm[2], r.n + 1)
                pe.wait_ge(s_nv[2], r.n + 1)
                turn(2, bank[6])

            def ffn2(r):
                pe.wait_ge(s_ev[2], r.n + 1)
                ffn(2, bank[5], s_f2)

            def near(r):
                it = r.n - NB
                pe.wait_ge(s_rep, it + 1)
                for m in range(M2):
                    for j in range(NBLK):
                        last = nc.tensor.transpose(bank[5 + m][:, j * P:(j + 1) * P], V[:, j, m * P:(m + 1) * P], ident[:])
                last.then_inc(s_nt, 1)
                pe.wait_ge(s_nin, it * 2 + 1)
                for m in range(M2):
                    for j in range(NBLK):
                        last = nc.tensor.matmul(bank[5 + m][:, j * P:(j + 1) * P], y[:, j, m * P:(m + 1) * P],
                                                tab[:, (Q + 3) * P:(Q + 4) * P], start=True, stop=True)
                last.then_inc(s_nt, 1)
                with pe.Fori(0, QT) as d:
                    c = it * QT + d
                    pe.wait_ge(s_nd, c * 7 + 1)
                    nc.tensor.matmul(bank[7][:], tab[:, (Q + 1) * P:(Q + 2) * P], pair_bc[:], start=True,
                                     stop=True).then_inc(s_ng, 1)
                pe.wait_ge(s_nin, it * 2 + 2)
                pe.wait_ge(s_nd, (it + 1) * (QT * 7))
                for j in range(NBLK):
                    for m in range(M2):
                        c = j % 2 * DI + m * P
                        last = nc.tensor.transpose(bank[5 + j // 2][:, c:c + P], near_y[:, m, j * P:(j + 1) * P], ident[:])
                last.then_inc(s_ny, 1)
                pe.wait_ge(s_near, it + 1)

            stages = [(carry, 2), (quarters(0), 2), (carry_last, 2), (quarters(1), 2), (pairs, 1), (ln1, 0),
                      (turn_b, 1), (turn_x(0), 1), (ffn1, 0), (turn_x(1), 1), (decay(0), 1), (turn_gated, 2),
                      (decay(1), 1), (project_out, 2), (ln2, 0), (project_bc, 0), (project_x, 0),
                      (project_z_dt(0), 0), (state, 1), (ln3, 2), (ffn2, 2), (project_z_dt(1), 0),
                      (project_z_dt(2), 0), (project_z_dt(3), 0)]
            by_row = [ln1, ffn1, ln2, project_bc, project_x, project_z_dt(0), project_z_dt(1), project_z_dt(2),
                      project_z_dt(3), pairs, turn_b, turn_x(0), turn_x(1), decay(0), decay(1), state, near, carry,
                      quarters(0), quarters(1), carry_last, turn_gated, project_out, ln3, ffn2]
            run(pe, stages)
            pe.wait_ge(s_low, 1)
            pe.wait_ge(s_yo, NB + 1)
            nc.tensor.matmul(bank[0][0:1, 0:P], lowest[:], ident[:], start=True, stop=True).then_inc(s_wt1, 1)
            run_again(pe, by_row, lambda: pe.wait_ge(s_gt, 1))

        @block.scalar
        def _(act):
            def rsqrt(L):
                def f(r):
                    act.wait_ge(s_mv[L], r.n + 1)
                    nc.scalar.activation(lnv[:, L, :], mv[:, L, :, 1], ACT.Ln, bias=eps[:]).then_inc(s_lv[L], 1)
                    act.wait_ge(s_lv[L], r.n + 1)
                    nc.scalar.activation(rstd[:, L, :], lnv[:, L, :], ACT.Exp, scale=-0.5).then_inc(s_rs[L], 1)
                return f

            def copy_turned(L, bk):
                def f(r):
                    act.wait_ge(s_tr[L], r.n + 1)
                    nc.scalar.copy(xnT[:, L, :], bank[bk][:]).then_inc(s_ev[L], 1)
                return f

            def normalise(L, src):
                def f(r):
                    act.wait_ge(s_nb[L], r.n + 1)
                    for j in range(NBLK // 2):
                        last = nc.scalar.activation(xn[:, L, j, :], src(r)[:, j, :], ACT.Identity, scale=rstd[:, L, j:j + 1],
                                                    bias=neg_mr[:, L, j:j + 1])
                    last.then_inc(s_nm[L], 1)
                return f

            def copy_bc(r):
                act.wait_ge(s_bc, r.n * 2 + 1)
                nc.scalar.copy(BT[:, r.s, :], bank[0][:]).then_inc(s_bce, 1)
                act.wait_ge(s_bc, r.n * 2 + 2)
                nc.scalar.copy(CT[:, r.s, :], bank[1][:]).then_inc(s_bce, 1)

            def first_tap(r):
                first(act, r, s_load["col"])
                for m, bk in enumerate((2, 0)):
                    act.wait_ge(s_px, r.n * 2 + m + 1)
                    nc.scalar.activation(xc[:, m, :], bank[bk][:], ACT.Identity, scale=col[:, m, TAPS - 1:TAPS],
                                         bias=col[:, m, TAPS:TAPS + 1]).then_inc(s_c0, 1)

            def silu_x(r):
                for m in range(M2):
                    act.wait_ge(s_cv, r.n * 6 + 5 + m)
                    last = nc.scalar.activation(xT[:, r.s, m, :], xc[:, m, :], ACT.Silu)
                last.then_inc(s_sx, 1)

            def silu_z(j):
                def block_j(r):
                    act.wait_ge(s_pz, r.n * NBLK + j + 1)
                    nc.scalar.activation(sz[:, r.s, j, :], bank[(1, 2, 0, 1)[j]][:, 0:DI], ACT.Silu).then_inc(s_sz, 1)
                return block_j

            def exp_ln_table(r):
                nc.scalar.preload_act_table_set(EXP_LN)

            def softplus(r):
                act.wait_ge(s_v, r.n * NBLK + NBLK)
                nc.scalar.activation(dtv[:, 1, :], dtv[:, 0, :], ACT.Abs).then_inc(s_sp, 1)
                act.wait_ge(s_sp, r.n * 3 + 1)
                nc.scalar.activation(dtv[:, 2, :], dtv[:, 1, :], ACT.Exp, scale=-1.0).then_inc(s_sp, 1)
                act.wait_ge(s_sp, r.n * 3 + 2)
                nc.scalar.activation(dtv[:, 3, :], dtv[:, 2, :], ACT.Ln, bias=ones[:]).then_inc(s_sp, 1)

            def a_part(i):
                def part_i(r):
                    if i == 0:
                        act.wait_ge(s_a, r.n + 1)
                        nc.scalar.copy(a3[:, r.s, 0, :], a[:, r.s, :]).then_inc(s_a3, 1)
                    else:
                        act.wait_ge(s_ar, r.n * 2 + i)
                        nc.scalar.copy(a3[:, r.s, i, :], a_rest[:, i - 1, :]).then_inc(s_a3, 1)
                return part_i

            def copy_b(r):
                act.wait_ge(s_bt, r.n + 1)
                nc.scalar.copy(Btm[:], bank[4][:, 0:(NBLK - 1) * P].rearrange("p (j n) -> p j n", n=P)).then_inc(s_bte, 1)

            def copy_x(i):
                def half_i(r):
                    act.wait_ge(s_bx, r.n * 2 + i + 1)
                    nc.scalar.copy(Xtm[:, 2 * i:2 * i + 2, :],
                                   bank[3 + i][:].rearrange("p (j c) -> p j c", c=DI)).then_inc(s_bxe, 1)
                return half_i

            def exp_source(r):
                act.wait_ge(s_cl, r.n + 1)
                nc.scalar.activation(Ed[:], Dc[:, 0:Q], ACT.Exp).then_inc(s_eD, 1)

            def exp_block(r):
                act.wait_ge(s_wst, r.n + 2)
                nc.scalar.activation(Eb[:, r.s, 0:3].rearrange("p i j h -> p (i j h)"), bank[4][:, 0:3 * P], ACT.Exp)
                nc.scalar.activation(Eb[:, r.s, 3].rearrange("p j h -> p (j h)"), Dc[:, Q], ACT.Exp).then_inc(s_eT, 1)

            def first_state(r):
                act.wait_ge(s_H, r.n * 4 + 2)
                nc.scalar.copy(St[:, 0, :], bank[3][:, 0:DI]).then_inc(s_st0, 1)

            def squares(g):
                def half_g(r):
                    act.wait_ge(s_yr, r.n * 2 + g + 1)
                    for j in (2 * g, 2 * g + 1):
                        last = nc.scalar.activation(sq[:, j, :], y[:, j, :], ACT.Square, accum_out=ssq[:, j:j + 1])
                    last.then_inc(s_sq, 1)
                return half_g

            def copy_gated(m):
                def half_m(r):
                    act.wait_ge(s_yt, r.n * 2 + m + 1)
                    nc.scalar.copy(ygT[:, m, :], bank[5 + m][:]).then_inc(s_yte, 1)
                return half_m

            def rms(r):
                act.wait_ge(s_sq, r.n * 2 + 2)
                nc.scalar.activation(lny[:], ssq[:], ACT.Ln, scale=1.0 / DI, bias=eps[:]).then_inc(s_lry, 1)
                act.wait_ge(s_lry, r.n + 1)
                nc.scalar.activation(ry[:], lny[:], ACT.Exp, scale=-0.5).then_inc(s_ry, 1)

            nc.scalar.preload_act_table_set(EXP_LN)
            act.wait_ge(s_eps, 1)

            def decay_rates(r):
                if isinstance(r.n, int) and r.n == 0:
                    act.wait_ge(s_load["row"], 16)
                    nc.scalar.activation(pos_a[:], row[:, 2 * P:2 * P + H], ACT.Exp).then_inc(s_pa, 1)

            def near(r):
                with act.Fori(0, QT) as d:
                    c = (r.n - NB) * QT + d
                    act.wait_ge(s_nd, c * 7 + 3)
                    nc.scalar.activation(near_e[:], near_d[:], ACT.Exp).then_inc(s_ne, 1)

            stages = [(silu_z(2), 1), (first_state, 2), (silu_z(3), 1), (exp_ln_table, 1), (rsqrt(0), 0),
                      (softplus, 1), (normalise(0, lambda r: x_in[:, r.s]), 0), (a_part(0), 1),
                      (copy_turned(0, 0), 0), (a_part(1), 1), (squares(0), 2), (copy_b, 1), (copy_x(0), 1),
                      (decay_rates, 0), (a_part(2), 1), (squares(1), 2), (copy_x(1), 1), (copy_gated(0), 2),
                      (copy_gated(1), 2), (rsqrt(1), 0), (rms, 2), (exp_source, 1), (exp_block, 1),
                      (normalise(1, lambda r: h1[:, r.s]), 0), (copy_turned(1, 0), 0), (copy_bc, 0), (rsqrt(2), 2),
                      (first_tap, 0), (normalise(2, lambda r: h2), 2), (silu_z(0), 0), (copy_turned(2, 6), 2),
                      (silu_x, 0), (silu_z(1), 0)]
            by_row = [rsqrt(0), normalise(0, lambda r: x_in[:, r.s]), copy_turned(0, 0), rsqrt(1),
                      normalise(1, lambda r: h1[:, r.s]), copy_turned(1, 0), copy_bc, first_tap, silu_x, silu_z(0),
                      silu_z(1), silu_z(2), silu_z(3), exp_ln_table, softplus, a_part(0), a_part(1), a_part(2),
                      copy_b, copy_x(0), copy_x(1), exp_source, exp_block, first_state, near, squares(0),
                      squares(1), rms, copy_gated(0), copy_gated(1), rsqrt(2), normalise(2, lambda r: h2),
                      copy_turned(2, 6)]
            run(act, stages)
            run_again(act, by_row)

        @block.vector
        def _(dve):
            def meanvar(L, src, r):
                for j in range(NBLK):
                    last = nc.vector.bn_stats(stats[:, L, j, :], src[:, j, :])
                last.then_inc(s_st[L], 1)
                dve.wait_ge(s_st[L], r.n * 3 + 1)
                nc.vector.tensor_tensor(pair[:, L, :, 0:2], stats[:, L, :, 1:3], stats[:, L, :, 4:6], ALU.add)
                nc.vector.tensor_tensor(pair[:, L, :, 2], stats[:, L, :, 1], stats[:, L, :, 4],
                                        ALU.subtract).then_inc(s_st[L], 1)
                dve.wait_ge(s_st[L], r.n * 3 + 2)
                nc.vector.scalar_tensor_tensor(out=pair[:, L, :, 3], in0=pair[:, L, :, 2], scalar=0.25,
                                               in1=pair[:, L, :, 2], op0=ALU.mult, op1=ALU.mult)
                nc.vector.tensor_scalar(mv[:, L, :, 0], pair[:, L, :, 0], -0.5, None, ALU.mult).then_inc(s_st[L], 1)
                dve.wait_ge(s_st[L], r.n * 3 + 3)
                nc.vector.scalar_tensor_tensor(out=mv[:, L, :, 1], in0=pair[:, L, :, 1], scalar=1.0 / P,
                                               in1=pair[:, L, :, 3], op0=ALU.mult, op1=ALU.add).then_inc(s_mv[L], 1)

            def scaled_mean(L):
                def f(r):
                    dve.wait_ge(s_rs[L], r.n + 1)
                    nc.vector.tensor_tensor(neg_mr[:, L, :], mv[:, L, :, 0], rstd[:, L, :], ALU.mult).then_inc(s_nb[L], 1)
                return f

            def normalise(L, src):
                def f(r):
                    for j in range(NBLK // 2, NBLK):
                        last = nc.vector.tensor_scalar(xn[:, L, j, :], src(r)[:, j, :], mv[:, L, j, 0:1],
                                                       rstd[:, L, j:j + 1], ALU.add, ALU.mult)
                    last.then_inc(s_nv[L], 1)
                return f

            def ln1_stats(r):
                dve.wait_ge(s_x[r.s], (r.k + 1) * 16)
                meanvar(0, x_in[:, r.s], r)

            def ffn1(r):
                dve.wait_ge(s_f1, r.n + 1)
                dve.wait_ge(s_xb, r.n + 1)
                nc.vector.tensor_tensor(h1[:, r.s], bank[1][:].rearrange("p (j d) -> p j d", d=P), xb[:],
                                        ALU.add).then_inc(s_h1, 1)
                dve.wait_ge(s_h1, r.n + 1)
                meanvar(1, h1[:, r.s], r)

            def conv(r):
                for k in range(1, TAPS):
                    for m in range(M2):
                        if k == 1:
                            dve.wait_ge(s_c0, r.n * 2 + m + 1)
                        else:
                            dve.wait_ge(s_cv, r.n * 6 + (k - 2) * 2 + m + 1)
                        nc.vector.scalar_tensor_tensor(
                            out=xc[:, m, k:T], in0=bank[(2, 0)[m]][:, 0:T - k], scalar=col[:, m, TAPS - 1 - k:TAPS - k],
                            in1=xc[:, m, k:T], op0=ALU.mult, op1=ALU.add).then_inc(s_cv, 1)

            def dt_bias(j):
                def block_j(r):
                    dve.wait_ge(s_pz, r.n * NBLK + j + 1)
                    dve.wait_ge(s_sz, r.n * NBLK + j + 1)
                    nc.vector.tensor_tensor(dtv[:, 0, j * H:(j + 1) * H], bank[(1, 2, 0, 1)[j]][:, DI:DI + H],
                                            row[:, 2 * P + H:2 * P + 2 * H], ALU.add).then_inc(s_v, 1)
                return block_j

            def dt_and_a(r):
                dve.wait_ge(s_sp, r.n * 3 + 3)
                nc.vector.scalar_tensor_tensor(out=dt[:, r.s, :], in0=dtv[:, 0, :], scalar=0.0, in1=dtv[:, 3, :],
                                               op0=ALU.max, op1=ALU.add).then_inc(s_dt, 1)
                dve.wait_ge(s_dt, r.n + 1)
                nc.vector.tensor_tensor(a[:, r.s, :].rearrange("p (j h) -> p j h", h=H),
                                        dt[:, r.s, :].rearrange("p (j h) -> p j h", h=H),
                                        neg_a[:].unsqueeze(1).to_broadcast([P, NBLK, H]), ALU.mult).then_inc(s_a, 1)

            def mask_g(r):
                dve.wait_ge(s_G, r.n + 1)
                wait(dve, s_Z1, r.n * 2)
                nc.vector.tensor_tensor(Gm[:], bank[3][:].rearrange("p (j t) -> p j t", t=P),
                                        MASK.unsqueeze(1).to_broadcast([P, NBLK, P]), ALU.mult).then_inc(s_gm, 1)

            def clamp(r):
                dve.wait_ge(s_D, r.n * 2 + 1)
                nc.vector.tensor_scalar(Dc[:, 0:Q], bank[3][:].rearrange("p (q c) -> p q c", q=Q), CLAMP, None,
                                        ALU.min).then_inc(s_cl, 1)

            def clamp_block(r):
                dve.wait_ge(s_D, r.n * 2 + 2)
                nc.vector.tensor_scalar(Dc[:, Q], bank[4][:, 3 * P:], CLAMP, None, ALU.min)
                dve.wait_ge(s_wst, r.n + 1)
                nc.vector.tensor_tensor(worst[:], worst[:], bank[4][:, 3 * P:], ALU.min).then_inc(s_wst, 1)

            def weigh(r):
                dve.wait_ge(s_bxe, r.n * 2 + 2)
                dve.wait_ge(s_wt, r.n * 2 + 2)
                for j in range(NBLK - 1):
                    last = scale_x(nc.vector, r, slice(0, Q), Q, j)
                last.then_inc(s_xd, 1)

            def states(r):
                s0, s1, s2 = bank[3][:, 0:DI], bank[3][:, DI:2 * DI], bank[4][:, 0:DI]
                dve.wait_ge(s_S, r.n + 1)

                def by_head(ap):
                    return ap.rearrange("p (h e) -> p h e", e=HD)

                def decayed(dst, src, j):
                    return nc.vector.tensor_tensor(by_head(dst), by_head(src),
                                                   Eb[:, r.s, 1, j, :].unsqueeze(2).to_broadcast([P, H, HD]), ALU.mult)
                decayed(Sd[:, 0, :], s0, 1).then_inc(s_H, 1)
                dve.wait_ge(s_H, r.n * 4 + 1)
                nc.vector.tensor_tensor(St[:, 1, :], Sd[:, 0, :], s1, ALU.add).then_inc(s_H, 1)
                dve.wait_ge(s_H, r.n * 4 + 2)
                decayed(Sd[:, 1, :], St[:, 1, :], 2).then_inc(s_H, 1)
                dve.wait_ge(s_H, r.n * 4 + 3)
                nc.vector.tensor_tensor(St[:, 2, :], Sd[:, 1, :], s2, ALU.add).then_inc(s_H, 1)

            def times(out, product, i, js, r):
                return nc.vector.tensor_tensor(
                    out[:, js, :].rearrange("p j (h e) -> p j h e", e=HD),
                    product.rearrange("p (j h e) -> p j h e", e=HD, h=H),
                    Eb[:, r.s, i, js, :].unsqueeze(3).to_broadcast([P, js.stop - js.start, H, HD]), ALU.mult)

            def scale_carry(r):
                dve.wait_ge(s_Z2, r.n * 2 + 1)
                times(Tm, bank[7][:], 2, slice(1, 3), r).then_inc(s_T, 1)

            def scale_carry_last(r):
                dve.wait_ge(s_Z2, r.n * 2 + 2)
                times(Tm, bank[7][:, 0:DI], 2, slice(3, 4), r).then_inc(s_T, 1)

            def scale_quarters(g):
                def half_g(r):
                    dve.wait_ge(s_Z1, r.n * 2 + g + 1)
                    times(V, bank[5 + g][:], 3, slice(2 * g, 2 * g + 2), r).then_inc(s_y, 1)
                return half_g

            def sum_y(g):
                def half_g(r):
                    js = slice(2 * g, 2 * g + 2)
                    dve.wait_ge(s_y, r.n * 2 + g + 1)
                    dve.wait_ge(s_TD, r.n * 2 + g + 1)
                    nc.vector.tensor_tensor(y[:, js, :], V[:, js, :], TD[:, js, :], ALU.add).then_inc(s_yr, 1)
                return half_g

            def residual2(r):
                dve.wait_ge(s_po, r.n + 1)
                dve.wait_ge(s_ry, r.n + 1)
                for j in range(NBLK):
                    last = nc.vector.scalar_tensor_tensor(out=h2[:, j, :], in0=bank[7][:, j * P:(j + 1) * P],
                                                          scalar=ry[:, j:j + 1], in1=h1[:, r.s, j, :],
                                                          op0=ALU.mult, op1=ALU.add)
                last.then_inc(s_h2, 1)
                dve.wait_ge(s_h2, r.n + 1)
                meanvar(2, h2[:], r)

            def finish(r):
                dve.wait_ge(s_f2, r.n + 1)
                dve.wait_ge(s_h2b, r.n + 1)
                dve.wait_ge(s_out[r.s], (r.k + 1) * 16)
                nc.vector.tensor_tensor(y_out[:, r.s], bank[5][:].rearrange("p (j d) -> p j d", d=P), h2b[:],
                                        ALU.add).then_inc(s_yo, 1)

            nc.vector.memset(ones[:], 1.0)
            nc.vector.memset(Tm[:, 0, :], 0.0)
            nc.vector.memset(eps[:], EPS).then_inc(s_eps, 1)
            nc.vector.memset(worst[:], 0.0).then_inc(s_wst, 1)

            def ffn_weights(r):
                if isinstance(r.n, int) and r.n == 0:
                    dve.wait_ge(s_load["w_ffn"], 16)
                    dve.wait_ge(s_load["row"], 16)
                    nc.vector.scalar_tensor_tensor(out=scaled_ffn[:], in0=w_ffn[:], scalar=0.5 / 127.0, in1=row[:, 0:P],
                                                   op0=ALU.mult, op1=ALU.mult).then_inc(s_wr, 1)
                    nc.vector.tensor_scalar(half_bias[:], row[:, P:2 * P], 0.5, None, ALU.mult).then_inc(s_wr, 1)

            def other_weights(r):
                if isinstance(r.n, int) and r.n == 0:
                    dve.wait_ge(s_load["tab"], 16)
                    nc.vector.tensor_copy(sums[:], tab[:, 0:NSUM * P].rearrange("p (i s) -> p i s", s=P)).then_inc(s_wr, 1)
                    dve.wait_ge(s_load["col"], 16)
                    dve.wait_ge(s_load["w_out"], 16)
                    for m in range(M2):
                        last = nc.vector.tensor_scalar(scaled_out[:, m, :], w_out[:, m, :], col[:, m, TAPS + 1:TAPS + 2],
                                                       None, ALU.mult)
                    last.then_inc(s_wr, 1)
                    dve.wait_ge(s_pa, 1)
                    nc.vector.tensor_scalar(neg_a[:], pos_a[:], -1.0, None, ALU.mult).then_inc(s_wr, 1)
                    dve.wait_ge(s_wr, 5)

            def near(r):
                it = r.n - NB
                dve.wait_ge(s_XD, r.n + 1)
                by_head = "p j (h e) -> p j h e"

                def spread(v):
                    return v[:, r.s, :].rearrange("p (j h) -> p j h", h=H).unsqueeze(3).to_broadcast([P, NBLK, H, HD])
                nc.vector.tensor_tensor(V[:].rearrange(by_head, e=HD), Xtm[:].rearrange(by_head, e=HD), spread(dt), ALU.mult)
                nc.vector.tensor_copy(y[:].rearrange(by_head, e=HD), spread(a)).then_inc(s_rep, 1)
                nc.vector.tensor_copy(b_pad[:, QT:], BT[:, r.s, :])
                nc.vector.memset(distance[:], 0.0)
                for k, target in enumerate((xdt_pad, cum_pad)):
                    dve.wait_ge(s_nt, it * 2 + k + 1)
                    for m in range(M2):
                        last = nc.vector.tensor_copy(target[:, m, QT:], bank[5 + m][:])
                    last.then_inc(s_nin, 1)
                dve.wait_ge(s_nin, it * 2 + 2)
                nc.vector.memset(near_y[:], 0.0)
                with dve.Fori(0, QT) as d:
                    c = it * QT + d
                    back = bass.ds(QT - d, T)
                    nc.vector.tensor_tensor(pair_bc[:], CT[:, r.s, :], b_pad[:, back], ALU.mult).then_inc(s_nd, 1)
                    nc.vector.tensor_tensor(near_d[:], cum_pad[:, :, QT:], cum_pad[:, :, back], ALU.subtract).then_inc(s_nd, 1)
                    dve.wait_ge(s_nd, c * 7 + 2)
                    nc.vector.tensor_scalar(near_d[:], near_d[:], 0.0, None, ALU.min).then_inc(s_nd, 1)
                    dve.wait_ge(s_ne, c + 1)
                    nc.vector.scalar_tensor_tensor(out=near_e[:], in0=place_row[:].unsqueeze(1).to_broadcast([P, M2, T]),
                                                   scalar=distance[:], in1=near_e[:], op0=ALU.is_ge,
                                                   op1=ALU.mult).then_inc(s_nd, 1)
                    dve.wait_ge(s_nd, c * 7 + 4)
                    nc.vector.tensor_tensor(near_e[:], near_e[:], xdt_pad[:, :, back], ALU.mult).then_inc(s_nd, 1)
                    nc.vector.tensor_scalar(distance[:], distance[:], 1.0, None, ALU.add)
                    dve.wait_ge(s_nd, c * 7 + 5)
                    dve.wait_ge(s_ng, c + 1)
                    nc.vector.tensor_tensor(near_e[:], near_e[:], bank[7][:].unsqueeze(1).to_broadcast([P, M2, T]),
                                            ALU.mult).then_inc(s_nd, 1)
                    dve.wait_ge(s_nd, c * 7 + 6)
                    nc.vector.tensor_tensor(near_y[:], near_y[:], near_e[:], ALU.add).then_inc(s_nd, 1)
                    dve.wait_ge(s_nd, c * 7 + 7)
                dve.wait_ge(s_ny, it + 1)
                for g in range(2):
                    last = nc.vector.tensor_tensor(XD[:, r.s, 2 * g:2 * g + 2, :], XD[:, r.s, 2 * g:2 * g + 2, :],
                                                   bank[5 + g][:].rearrange("p (j c) -> p j c", c=DI), ALU.add)
                last.then_inc(s_near, 1)

            def general_tables():
                dve.wait_ge(s_load["general_tab"], 16)
                dve.wait_ge(s_load["place"], 16)
                nc.vector.memset(b_pad[:, 0:QT], 0.0)
                nc.vector.memset(cum_pad[:, :, 0:QT], 0.0)
                nc.vector.memset(xdt_pad[:, :, 0:QT], 0.0)
                nc.vector.tensor_copy(sums[:], tab[:, 0:NSUM * P].rearrange("p (i s) -> p i s", s=P)).then_inc(s_gt, 1)

            stages = [(ln1_stats, 0), (scale_carry, 2), (ffn_weights, 0), (dt_bias(1), 1), (dt_bias(2), 1),
                      (dt_bias(3), 1), (scaled_mean(0), 0), (normalise(0, lambda r: x_in[:, r.s]), 0),
                      (other_weights, 0), (scale_carry_last, 2), (scale_quarters(0), 2), (dt_and_a, 1),
                      (sum_y(0), 2), (mask_g, 1), (scale_quarters(1), 2), (sum_y(1), 2), (ffn1, 0), (clamp, 1),
                      (clamp_block, 1), (scaled_mean(1), 0), (normalise(1, lambda r: h1[:, r.s]), 0),
                      (residual2, 2), (weigh, 1), (scaled_mean(2), 2), (normalise(2, lambda r: h2), 2), (conv, 0),
                      (dt_bias(0), 0), (states, 1), (finish, 2)]
            by_row = [ln1_stats, scaled_mean(0), normalise(0, lambda r: x_in[:, r.s]), ffn1, scaled_mean(1),
                      normalise(1, lambda r: h1[:, r.s]), conv, dt_bias(0), dt_bias(1), dt_bias(2), dt_bias(3),
                      dt_and_a, mask_g, clamp, clamp_block, weigh, states, near, scale_carry, scale_quarters(0),
                      scale_carry_last, scale_quarters(1), sum_y(0), sum_y(1), residual2, scaled_mean(2),
                      normalise(2, lambda r: h2), finish]
            run(dve, stages)
            dve.wait_ge(s_wst, NB + 1)
            nc.vector.tensor_reduce(lowest[:], worst[:], AX_X, ALU.min).then_inc(s_low, 1)
            dve.wait_ge(s_wt1, 1)
            nc.vector.tensor_reduce(low[0:1, :], bank[0][0:1, 0:P], AX_X, ALU.min).then_inc(s_low, 1)
            dve.wait_ge(s_low, 2)
            nc.vector.tensor_scalar(flag[0:1, :], low[0:1, :], -LIMIT / 2, None, ALU.is_lt).then_inc(s_flag, 1)
            run_again(dve, by_row, general_tables)

        @block.gpsimd
        def _(pool):
            def bias1(r):
                pool.wait_ge(s_x[r.s], (r.k + 1) * 16)
                wait(pool, s_h1, r.n)
                first(pool, r, s_wr, 2)
                nc.gpsimd.tensor_tensor(xb[:], x_in[:, r.s], half_bias[:].unsqueeze(1).to_broadcast([P, NBLK, P]),
                                        ALU.add).then_inc(s_xb, 1)

            def a_left(i):
                def rest_i(r):
                    pool.wait_ge(s_a3, r.n * 3 + i + 1)
                    src = a[:, r.s, :] if i == 0 else a_rest[:, 0, :]
                    nc.gpsimd.tensor_tensor(a_rest[:, i, :], src, a3[:, r.s, i, :], ALU.subtract).then_inc(s_ar, 1)
                return rest_i

            def source_weights(r):
                pool.wait_ge(s_eD, r.n + 1)
                wait(pool, s_xd, r.n)
                nc.gpsimd.tensor_tensor(Wt[:, 0:Q].rearrange("p q j h -> p q (j h)"), Ed[:],
                                        dt[:, r.s, :].unsqueeze(1).to_broadcast([P, Q, NBLK * H]), ALU.mult).then_inc(s_wt, 1)
                pool.wait_ge(s_eT, r.n + 1)
                nc.gpsimd.tensor_tensor(Wt[:, Q].rearrange("p j h -> p (j h)"),
                                        Eb[:, r.s, 0].rearrange("p j h -> p (j h)"), dt[:, r.s, :],
                                        ALU.mult).then_inc(s_wt, 1)

            def weigh_to_end(r):
                pool.wait_ge(s_wt, r.n * 2 + 2)
                pool.wait_ge(s_bxe, r.n * 2 + 2)
                for j in range(NBLK - 1):
                    last = scale_x(nc.gpsimd, r, slice(Q, Q + 1), 1, j)
                last.then_inc(s_xe, 1)

            def weigh_last(r):
                scale_x(nc.gpsimd, r, slice(0, Q), Q, NBLK - 1).then_inc(s_xp, 1)

            def skip(r):
                pool.wait_ge(s_bxe, r.n * 2 + 2)
                nc.gpsimd.tensor_tensor(XD[:, r.s], Xtm[:], row[:, 2 * P + 2 * H:].unsqueeze(1).to_broadcast([P, NBLK, DI]),
                                        ALU.mult).then_inc(s_XD, 1)

            def carried(g):
                def half_g(r):
                    js = slice(2 * g, 2 * g + 2)
                    pool.wait_ge(s_XD, r.n + 1)
                    wait(pool, s_yr, r.n * 2)
                    pool.wait_ge(s_T, r.n * 2 + g + 1)
                    nc.gpsimd.tensor_tensor(TD[:, js, :], Tm[:, js, :], XD[:, r.s, js, :], ALU.add).then_inc(s_TD, 1)
                return half_g

            def gate(g):
                def half_g(r):
                    js = slice(2 * g, 2 * g + 2)
                    pool.wait_ge(s_yr, r.n * 2 + g + 1)
                    nc.gpsimd.tensor_tensor(yg[:, js, :], y[:, js, :], sz[:, r.s, js, :], ALU.mult).then_inc(s_yg, 1)
                return half_g

            def bias2(r):
                pool.wait_ge(s_h2, r.n + 1)
                nc.gpsimd.tensor_tensor(h2b[:], h2[:], half_bias[:].unsqueeze(1).to_broadcast([P, NBLK, P]),
                                        ALU.add).then_inc(s_h2b, 1)

            def near(r):
                pool.wait_ge(s_near, r.n - NB + 1)

            stages = [(weigh_to_end, 2), (bias1, 0), (weigh_last, 2), (carried(0), 2), (carried(1), 2),
                      (a_left(0), 1), (gate(0), 2), (a_left(1), 1), (gate(1), 2), (source_weights, 1), (skip, 1),
                      (bias2, 2)]
            by_row = [bias1, a_left(0), a_left(1), skip, source_weights, weigh_to_end, weigh_last, near,
                      carried(0), carried(1), gate(0), gate(1), bias2]
            run(pool, stages)
            run_again(pool, by_row)


def kernel(L0_attn_x, L0_attn_in_proj_w, L0_attn_conv_w, L0_attn_conv_b, L0_attn_A_log, L0_attn_Dp,
           L0_attn_dt_bias, L0_attn_norm_w, L0_attn_out_proj_w, L0_ffn_CB, L0_ffn_SCB, L0_ffn_bias):
    import concourse.bacc as bacc
    from concourse.bass_utils import run_bass_kernel_spmd

    def inner(v):
        v = np.asarray(v)
        return v.reshape(M2, P, -1).transpose(1, 0, 2)

    w_in = np.asarray(L0_attn_in_proj_w).T
    arrays = {
        "x": L0_attn_x,
        "w_in_t": np.concatenate([w_in[:, :DI], w_in[:, 2 * DI:2 * DI + 2 * P], w_in[:, DI:2 * DI],
                                  w_in[:, 2 * DI + 2 * P:]], axis=1),
        "w_ffn_t": np.asarray(L0_ffn_CB).T,
        "w_out_t": inner(np.asarray(L0_attn_out_proj_w).T),
        "rows": np.concatenate([np.asarray(v) for v in (L0_ffn_SCB, L0_ffn_bias, L0_attn_A_log, L0_attn_dt_bias,
                                                        np.repeat(np.asarray(L0_attn_Dp), HD))]),
        "cols": np.concatenate([inner(L0_attn_conv_w), inner(L0_attn_conv_b), inner(L0_attn_norm_w)], axis=2),
        "tabs": np.stack([tables(False), tables(True)]),
        "eye": np.eye(P, dtype=np.float32),
        "place": (np.arange(T) % QT).astype(np.float32),
    }
    arrays = {k: np.ascontiguousarray(v) for k, v in arrays.items()}
    nc = bacc.Bacc("TRN2", target_bir_lowering=False, num_devices=1)
    args = [nc.dram_tensor(k, v.shape, mybir.dt.from_np(v.dtype), kind="ExternalInput").ap() for k, v in arrays.items()]
    args.append(nc.dram_tensor("out", arrays["x"].shape, F32, kind="ExternalOutput").ap())
    build(nc, *args)
    r = run_bass_kernel_spmd(nc, [arrays], core_ids=[0])
    return r.results[0]["out"]
```
